# Optimizing a Trainium2 kernel written in Bass

```python
import numpy as np
import jax
import jax.numpy as jnp

def _softmax(x, axis=-1):
    return jax.nn.softmax(x, axis=axis)

def _gelu(x):
    return jax.nn.gelu(x, approximate=True)

def _silu(x):
    return jax.nn.silu(x)

def _sigmoid(x):
    return jax.nn.sigmoid(x)

def _layernorm(x, axis=-1, eps=1e-05):
    m = jnp.mean(x, axis=axis, keepdims=True)
    v = jnp.var(x, axis=axis, keepdims=True)
    return (x - m) / jnp.sqrt(v + eps)

def _scatter_add(tgt, idx, src, axis=0):
    return tgt.at[idx].add(src)

def _segment_sum(src, seg, n):
    return jax.ops.segment_sum(src, seg, n)
kernel_name = 'mk_sandwich_d1_jaxref_r4_4b1031'

def setup_inputs(seed: int=0):
    np.random.seed(seed)
    _w = jnp.asarray

    def _L0_attn_setup():
        import jax, jax.numpy as jnp
        import numpy as np
        EPS = 1e-05
        key = jax.random.key(seed)
        ks = jax.random.split(key, 6)
        B, T, H = (4, 512, 512)
        scale = 2 ** (-2.5) * (6.0 / (H + H)) ** 0.5
        return {'hidden_states': jax.random.normal(ks[0], (B, T, H), dtype=jnp.float32), 'Wi': jax.random.normal(ks[1], (H, H), dtype=jnp.float32) * scale, 'Wf': jax.random.normal(ks[2], (H, H), dtype=jnp.float32) * scale, 'Wg': jax.random.normal(ks[3], (H, H), dtype=jnp.float32) * scale, 'Wo': jax.random.normal(ks[4], (H, H), dtype=jnp.float32) * scale, 'gnorm_w': jnp.ones((H,), dtype=jnp.float32)}
    _L0_attn_in = _L0_attn_setup()

    def _L0_ffn_setup():
        import jax, jax.numpy as jnp
        import numpy as np
        B, S, D, H = (4, 512, 512, 2048)

        def fwht(x):
            orig_shape = x.shape
            n = orig_shape[-1]
            x = x.reshape(-1, n)
            h = 1
            while h < n:
                xb = x.reshape(-1, n // (2 * h), 2, h)
                a = xb[:, :, 0, :]
                b = xb[:, :, 1, :]
                x = jnp.stack([a + b, a - b], axis=2).reshape(-1, n)
                h *= 2
            scale = jnp.asarray(1.0 / np.sqrt(n), dtype=x.dtype)
            return (x * scale).reshape(orig_shape)
        key = jax.random.key(seed)
        kx, k1, k2, k3 = jax.random.split(key, 4)
        x = jax.random.normal(kx, (B, S, D), dtype=jnp.float32)
        W1 = jax.random.normal(k1, (H, D), dtype=jnp.float32) * (1.0 / np.sqrt(D))
        W2 = jax.random.normal(k2, (D, H), dtype=jnp.float32) * (1.0 / np.sqrt(H))
        W3 = jax.random.normal(k3, (H, D), dtype=jnp.float32) * (1.0 / np.sqrt(D))
        return {'x': x, 'W1': W1, 'W2': W2, 'W3': W3}
    _L0_ffn_in = _L0_ffn_setup()
    _d = {'L0_attn_hidden_states': _L0_attn_in['hidden_states'], 'L0_attn_Wi': _L0_attn_in['Wi'], 'L0_attn_Wf': _L0_attn_in['Wf'], 'L0_attn_Wg': _L0_attn_in['Wg'], 'L0_attn_Wo': _L0_attn_in['Wo'], 'L0_attn_gnorm_w': _L0_attn_in['gnorm_w'], 'L0_ffn_W1': _L0_ffn_in['W1'], 'L0_ffn_W2': _L0_ffn_in['W2'], 'L0_ffn_W3': _L0_ffn_in['W3']}
    _x0 = _d['L0_attn_hidden_states']
    _d['L0_attn_hidden_states'] = jax.random.normal(jax.random.fold_in(jax.random.key(seed), 1), (4, 512, 512), dtype=_x0.dtype)
    del _x0
    return _d

def reference(L0_attn_hidden_states, L0_attn_Wi, L0_attn_Wf, L0_attn_Wg, L0_attn_Wo, L0_attn_gnorm_w, L0_ffn_W1, L0_ffn_W2, L0_ffn_W3):

    def _L0_attn_ref(hidden_states, Wi, Wf, Wg, Wo, gnorm_w):
        import jax, jax.numpy as jnp
        import numpy as np
        EPS = 1e-05
        i = jnp.einsum('bth,dh->btd', hidden_states, Wi)
        f = jnp.einsum('bth,dh->btd', hidden_states, Wf)
        g = jnp.einsum('bth,dh->btd', hidden_states, Wg)
        gate = jax.nn.sigmoid(f)
        v = jax.nn.silu(i) * (1.0 - gate)

        def combine(c1, c2):
            a1, b1 = c1
            a2, b2 = c2
            return (a1 * a2, a2 * b1 + b2)
        _, o = jax.lax.associative_scan(combine, (gate, v), axis=1)
        rms = o * jax.lax.rsqrt(jnp.mean(o * o, axis=-1, keepdims=True) + EPS)
        o = rms * gnorm_w * g * jax.nn.sigmoid(g)
        return jnp.einsum('btd,hd->bth', o, Wo)

    def _L0_ffn_ref(x, W1, W2, W3):
        import jax, jax.numpy as jnp
        import numpy as np
        B, S, D, H = (4, 512, 512, 2048)

        def fwht(x):
            orig_shape = x.shape
            n = orig_shape[-1]
            x = x.reshape(-1, n)
            h = 1
            while h < n:
                xb = x.reshape(-1, n // (2 * h), 2, h)
                a = xb[:, :, 0, :]
                b = xb[:, :, 1, :]
                x = jnp.stack([a + b, a - b], axis=2).reshape(-1, n)
                h *= 2
            scale = jnp.asarray(1.0 / np.sqrt(n), dtype=x.dtype)
            return (x * scale).reshape(orig_shape)
        up_gate = jnp.einsum('bsd,hd->bsh', x, W1)
        up_lin = jnp.einsum('bsd,hd->bsh', x, W3)
        hidden = jax.nn.silu(up_gate) * up_lin
        hidden = fwht(hidden)
        out = jnp.einsum('bsh,dh->bsd', hidden, W2)
        return out
    x = L0_attn_hidden_states
    x = x + _layernorm(_L0_attn_ref(_layernorm(x, axis=-1), L0_attn_Wi, L0_attn_Wf, L0_attn_Wg, L0_attn_Wo, L0_attn_gnorm_w), axis=-1)
    x = x + _layernorm(_L0_ffn_ref(_layernorm(x, axis=-1), L0_ffn_W1, L0_ffn_W2, L0_ffn_W3), axis=-1)
    return x

_drawn_inputs = setup_inputs


def setup_inputs(seed=0):
    import zlib

    import numpy as np

    out = dict(_drawn_inputs(seed))
    spreads = {'L0_attn_gnorm_w': (1.0, 0.2)}
    factors = {}
    for name, (base, spread) in spreads.items():
        noise = np.random.default_rng([zlib.crc32(name.encode()), seed]).standard_normal(out[name].shape)
        drawn = base * np.exp(spread * noise) if base else spread * noise
        out[name] = jnp.asarray(drawn.astype(out[name].dtype))
    for name, factor in factors.items():
        out[name] = (out[name] * factor).astype(out[name].dtype)
    return out
```

```python
from contextlib import ExitStack

import numpy as np
import concourse.bass as bass
from concourse import mybir

ALU = mybir.AluOpType
ACT = mybir.ActivationFunctionType
AX = mybir.AxisListType
F32 = mybir.dt.float32
F16 = mybir.dt.float16
I32 = mybir.dt.int32
RMAX = bass.bass_isa.ReduceOp.max

P = 128
EPS = 1e-5
X_EXP = 11
ROW_EXP = 77
F_LEAST = 24
BIT = float(1 << 23)
NORM_BOUND_EXP = 9 + 29
HID_EXP = 15


def mixer_ffn_kernel(nc, x, w_i, w_f, w_g, w_o, gnorm, w_1, w_2, w_3, eye, hadamard, out):
    B, T, D = x.shape
    H = w_1.shape[0]
    KC = D // P
    TC = T // P
    HC = H // P
    HQ = HC // B
    assert T == D == 512 and KC == TC == B == 4 and HC == 16

    x_rows = x.rearrange("b (t p) d -> (b t) p d", p=P)
    out_rows = out.rearrange("b (t p) d -> (b t) p d", p=P)
    w1_rows = w_1.rearrange("(c p) d -> c p d", p=P)
    w3_rows = w_3.rearrange("(c p) d -> c p d", p=P)
    w2_rows = w_2.rearrange("(q p) h -> q p h", p=P)
    x1_rows = nc.dram_tensor("x1_rows", (B * TC, P, D), F32, kind="Internal").ap()
    x1t_dram = nc.dram_tensor("x1t_split", (B * TC, P, 2, KC, P), F16, kind="Internal").ap()

    with ExitStack() as ctx:
        def sb(name, shape, dt=F32, c=ctx):
            return c.enter_context(nc.sbuf_tensor(name, shape, dt))

        def sem(name):
            return ctx.enter_context(nc.semaphore(name))

        ident = sb("ident", [P, P])
        had = sb("had", [P, P])
        ones = sb("ones", [P, P])
        neg_half = sb("neg_half", [P, 1])
        gw = sb("gw", [P, KC])
        norm2 = sb("norm2", [P, 4, KC])
        row_s = sb("row_s", [P, 4, KC])
        row_inv = sb("row_inv", [P, 4, KC])
        unscale = sb("unscale", [P, 3, KC])
        g_coef = sb("g_coef", [P, KC])
        s_tmp = sb("s_tmp", [P, 8])
        y_inv = sb("y_inv", [P, 2])
        wn2 = sb("wn2", [P, 2])
        wexp = sb("wexp", [P, 2])
        w_s = sb("w_s", [P, 2])
        w13_inv = sb("w13_inv", [P, 2, HC])
        w2n2 = sb("w2n2", [P, 1])
        w2exp = sb("w2exp", [P, 1])
        w2_s = sb("w2_s", [P, 1])
        w2_inv = sb("w2_inv", [P, B])
        gate_c = sb("gate_c", [P, HC])
        up_c = sb("up_c", [P, HC])
        hid_s = sb("hid_s", [P, 4])
        st = sb("st", [P, 3, 6])
        mv = sb("mv", [P, 3, TC, 2])
        var = sb("var", [P, 3, TC])
        rstd = sb("rstd", [P, 3, TC])
        ab = sb("ab", [P, TC, 2])
        ms_eps = sb("ms_eps", [P, TC])
        w1t = sb("w1t", [P, 2, KC, H], F16)
        w3t = sb("w3t", [P, 2, KC, H], F16)
        w2t = sb("w2t", [P, 2, HC, D], F16)

        with ExitStack() as first:
            wft = sb("wft", [P, 2, KC, D], F16, first)
            wit = sb("wit", [P, 2, KC, D], F16, first)
            wgt = sb("wgt", [P, 2, KC, D], F16, first)
            wot = sb("wot", [P, 2, KC, D], F16, first)
            x_in = sb("x_in", [P, 2, D], F32, first)
            x_res = sb("x_res", [P, 2, D], F32, first)
            zn = sb("zn", [P, TC, D], F32, first)
            xnt = sb("xnt", [P, 2, KC, T], F16, first)
            ot = sb("ot", [P, 2, KC, T], F16, first)
            w_in = sb("w_in", [P, 2, D], F32, first)
            w2a = sb("w2a", [P, H], F32, first)
            w2b = sb("w2b", [P, H], F32, first)
            x1t_st = sb("x1t_st", [P, 2, 2, KC, P], F16, first)
            gate = sb("gate", [P, T], F32, first)
            sg = sb("sg", [P, 2, T], F32, first)
            sl = sb("sl", [P, T], F32, first)
            o_s = sb("o_s", [P, 2, T], F32, first)
            osum = sb("osum", [P, T], F32, first)
            osq = sb("osq", [P, T], F32, first)
            w_junk = sb("w_junk", [P, D], mybir.dt.bfloat16, first)[:]
            gs = sb("gs", [P, 2, T], F32, first)
        with ExitStack() as second:
            x2t = sb("x2t", [P, B, TC, 2, KC, P], F16, second)
            x1r = sb("x1r", [P, TC, D], F32, second)
            row_c = sb("row_c", [P, D], F32, second)
            diag = sb("diag", [P, B, P], F32, second)
            yv = sb("yv", [P, TC, D], F32, second)
            sga = sb("sga", [P, 2, T], F32, second)
            sil = sb("sil", [P, 2, T], F32, second)
            hd = sb("hd", [P, 2, T], F32, second)
            hsp = sb("hsp", [P, 2, 2, T], F16, second)

        ps = [ctx.enter_context(nc.psum_tensor(f"ps{i}", [P, 512], F32)) for i in range(8)]

        ld_eye, ld_had, ld_gw = sem("ld_eye"), sem("ld_had"), sem("ld_gw")
        ld_x, ld_res = ([sem(f"{s}{i}") for i in range(2)] for s in ("ld_x", "ld_res"))
        ld_w13, ld_w2, ld_x1r = sem("ld_w13"), sem("ld_w2"), sem("ld_x1r")
        ld_x2t = [sem(f"ld_x2t{i}") for i in range(B)]
        ld_aw = [sem(f"ld_aw{i}") for i in range(4)]
        st_x1, st_x1t = ([sem(f"{s}{i}") for i in range(2)] for s in ("st_x1", "st_x1t"))
        st_out = sem("st_out")
        ones_set, half_set = sem("ones_set"), sem("half_set")
        aw_sq, aw_scale, aw_mm, aw_hi, aw_lo = (sem(s) for s in (
            "aw_sq", "aw_scale", "aw_mm", "aw_hi", "aw_lo"))
        aw_srdy, w2_srdy = sem("aw_srdy"), sem("w2_srdy")
        part_max, all_max = sem("part_max"), sem("all_max")
        aw_chain, coef_chain, unscale_rdy, coef_rdy, yinv_rdy = (sem(s) for s in (
            "aw_chain", "coef_chain", "unscale_rdy", "coef_rdy", "yinv_rdy"))
        x_chain, x_var, x_rstd, x_norm, xt_mm, xt_hi, xt_lo = (sem(s) for s in (
            "x_chain", "x_var", "x_rstd", "x_norm", "xt_mm", "xt_hi", "xt_lo"))
        f_mm, i_mm, g_mm = sem("f_mm"), sem("i_mm"), sem("g_mm")
        gate_rdy, sgi_rdy, sgg_rdy, sli_rdy, nv_rdy, o_rdy, gs_rdy, op_rdy = (sem(s) for s in (
            "gate_rdy", "sgi_rdy", "sgg_rdy", "sli_rdy", "nv_rdy", "o_rdy", "gs_rdy", "op_rdy"))
        osq_rdy, oadd, o_hi, o_lo, ms_mm, e_rdy = (sem(s) for s in (
            "osq_rdy", "oadd", "o_hi", "o_lo", "ms_mm", "e_rdy"))
        y_mm, y_chain, y_var, y_rstd, y_ab, y_norm, x1_rdy = (sem(s) for s in (
            "y_mm", "y_chain", "y_var", "y_rstd", "y_ab", "y_norm", "x1_rdy"))
        y_scale = sem("y_scale")
        z_chain, z_var, z_rstd, z_norm, z_mm, z_hi, z_lo = (sem(s) for s in (
            "z_chain", "z_var", "z_rstd", "z_norm", "z_mm", "z_hi", "z_lo"))
        w_sq, w_chain, w_srdy, w_scaled, wt_mm, wt_hi, wt_lo = (sem(s) for s in (
            "w_sq", "w_chain", "w_srdy", "w_scaled", "wt_mm", "wt_hi", "wt_lo"))
        w2_sq, w2_chain, w2_scaled, w2_fly, w2t_mm, w2t_ev, h2_mm, h2_hi, h2_lo = (sem(s) for s in (
            "w2_sq", "w2_chain", "w2_scaled", "w2_fly", "w2t_mm", "w2t_ev", "h2_mm", "h2_hi", "h2_lo"))
        h_chain, hid_part, hid_max, hid_scale, diag_rdy, row_mm = (sem(s) for s in (
            "h_chain", "hid_part", "hid_max", "hid_scale", "diag_rdy", "row_mm"))
        ga_mm, up_mm, sga_rdy, sil_rdy, hid_rdy, hid_hi, hid_lo, d_mm = (sem(s) for s in (
            "ga_mm", "up_mm", "sga_rdy", "sil_rdy", "hid_rdy", "hid_hi", "hid_lo", "d_mm"))
        y_free, v_chain, v_var, v_rstd, v_ab, v_norm, out_rdy = (sem(s) for s in (
            "y_free", "v_chain", "v_var", "v_rstd", "v_ab", "v_norm", "out_rdy"))

        def gates(b, c, after_f=(), after_i=(), after_g=()):
            return [("F", b, c), *after_f, ("I", b, c), *after_i, ("G", b, c), *after_g, ("O", b, c)]

        def first_chunks(b, z=((),) * 5):
            return [("WN", b, 0)] + gates(
                b, 0,
                [("FW", b, 0), *z[0], ("WT", b, 0), ("WT", b, 1), ("WN", b, 1)],
                [("FW", b, 1), *z[1], ("WT", b, 2)],
                [*z[2], ("WT", b, 3), ("WN", b, 2), ("FW", b, 2)]
            ) + [("FW", b, 3)] + gates(
                b, 1,
                [*z[3], ("WT", b, 4), ("FW", b, 4)],
                [*z[4], ("WT", b, 5), ("WN", b, 3), ("FW", b, 5)],
                [("WT", b, 6), ("WT", b, 7), ("FW", b, 6)]) + [("FW", b, 7)]

        def last_chunks(b, last):
            n = b + 1
            more = [] if last else [("XL", n, 0), ("XL", n, 1)]
            stats = [] if last else [("X1", n, 0), ("X2", n, 0), ("X1", n, 1), ("X2", n, 1)]
            return more + gates(
                b, 2, [("W2T", b, 0), ("W2T", b, 1)], [("W2T", b, 2), ("W2T", b, 3)], [("H2", b, 0)]
            ) + gates(b, 3, [("H2", b, 1), ("H2", b, 2)], [("H2", b, 3)] + stats,
                      [] if last else [("W2N", n, 0)])

        def projection(b, last):
            n = b + 1
            x_a = [] if last else [("XT", n, 0), ("XT", n, 1)]
            x_b = [] if last else [("X1", n, 2), ("X2", n, 2), ("X1", n, 3), ("X2", n, 3)]
            return (x_a + [("MS", b, 0), ("Y", b, 0)] + x_b
                    + [("Y", b, 1), ("YN", b, 0)] + ([] if last else [("XT", n, 2)])
                    + [("Y", b, 2), ("Z1", b, 0), ("YN", b, 1)] + ([] if last else [("XT", n, 3)])
                    + [("Y", b, 3), ("Z2", b, 0), ("Z1", b, 1), ("YN", b, 2), ("Z2", b, 1)])

        def second_norm(b, last):
            more = lambda t: [] if last else [("RL", b + 1, t)]
            return ([("YN", b, 3), ("Z1", b, 2), ("ZT", b, 0)], [("Z2", b, 2), ("Z1", b, 3), ("ZT", b, 1)],
                    [("Z2", b, 3), ("ZT", b, 2), *more(0)], [("ZT", b, 3), *more(1)], [])

        def start():
            norm = [[("X1", 0, t), ("X2", 0, t)] for t in range(TC)]
            return (norm[0] + norm[1] + [("XT", 0, 0), ("XT", 0, 1)] + norm[2] + norm[3]
                    + [("XT", 0, 2), ("XT", 0, 3), ("AW", 0, 0), ("AW", 0, 1), ("AW", 0, 2), ("AO", 0, 0),
                       ("W2N", 0, 0), ("RL", 0, 0), ("RL", 0, 1)] + first_chunks(0))

        def middle(b, last=False):
            z = second_norm(b, last)
            rest = [s for part in z for s in part] if last else first_chunks(b + 1, z)
            return last_chunks(b, last) + projection(b, last) + rest

        def first_half(eng, part):
            def do(steps):
                for kind, b, t in steps:
                    if kind in part:
                        part[kind](b, t)
            do(start())
            with eng.Fori(0, B - 1) as b:
                do(middle(b))
            do(middle(B - 1, last=True))

        small = ("XT", "WT", "W2T", "H2", "ZT")
        uses = [s for s in start() + middle(0) + middle(1) + middle(2) + middle(3, True) if s[0] in small]
        bank_of = {s: 6 + n % 2 for n, s in enumerate(uses)}
        before = {s: uses[n - 2] for n, s in enumerate(uses) if n >= 2}
        for trip in range(1, B - 1):
            for (k, b, t), (_, b0, _) in zip(middle(trip), middle(0)):
                assert k not in small or bank_of[k, b, t] == bank_of[k, b0, t]

        def traced(b, b0=1):
            return b if isinstance(b, int) else b0

        def bank(kind, b, t):
            return ps[bank_of[kind, traced(b), t]]

        def quarters(bank_):
            return bank_[:].rearrange("p (k n) -> p k n", n=P)

        def first(b):
            return isinstance(b, int) and b == 0

        def passed(n, c):
            return n if isinstance(c, int) and c == 1 else n - 1

        def slot_uses(b, t):
            return TC // 2 * b + t // 2

        def row(ap, n):
            return ap[n] if isinstance(n, int) else ap[bass.ds(n, 1)].squeeze(0)

        block = ctx.enter_context(nc.Block())

        @block.sync
        def _(sp):
            sp.dma_start(ident[:], eye).then_inc(ld_eye, 16)
            for t in range(2):
                sp.dma_start(x_in[:, t], x_rows[t]).then_inc(ld_x[t], 16)
            staging = (w2a[:].rearrange("p (c d) -> p c d", c=KC), w2b[:].rearrange("p (c d) -> p c d", c=KC), zn)
            for w, src in enumerate((w_f, w_i, w_g)):
                sp.dma_start(staging[w][:, :, :], src.rearrange("(c p) d -> p c d", p=P)).then_inc(ld_aw[w], 16)

            def load_x(b, t):
                if not (first(b) and t < 2):
                    sp.wait_ge(xt_mm, TC * b + t - 1)
                sp.dma_start(x_in[:, t % 2], row(x_rows, TC * b + t)).then_inc(ld_x[t % 2], 16)

            def xt(b, t):
                if t < 2:
                    load_x(b, t + 2)

            def attention_weights(b, w):
                if w == 2:
                    sp.dma_start(gw[:], gnorm).then_inc(ld_gw, 16)
                    sp.dma_start(had[:], hadamard).then_inc(ld_had, 16)
                    sp.wait_ge(aw_mm, KC)
                    sp.dma_start(staging[0], w_o.rearrange("(c p) d -> p c d", p=P)).then_inc(ld_aw[3], 16)

            def load_w13(b, t):
                sp.wait_ge(wt_mm, 2 * (HQ * b + t))
                for w, rows in enumerate((w1_rows, w3_rows)):
                    sp.dma_start(w_in[:, w], row(rows, HQ * b + t)).then_inc(ld_w13, 16)

            def load_w2(b, t):
                if first(b):
                    sp.wait_ge(aw_mm, 4 * KC)
                else:
                    sp.wait_ge(w2t_mm, 4 * b)
                sp.dma_start(w2a[:], row(w2_rows, b)).then_inc(ld_w2, 16)

            def load_res(b, t):
                if not (first(b) and t < 2):
                    sp.wait_ge(st_x1[t % 2], 16 * slot_uses(b, t))
                    sp.wait_ge(z_norm, TC * b + t - 1)
                    if t < 2:
                        sp.wait_ge(st_x1t[t % 2], 16 * slot_uses(b, t))
                sp.dma_start(x_res[:, t % 2], row(x_rows, TC * b + t)).then_inc(ld_res[t % 2], 16)

            def yn(b, t):
                sp.wait_ge(x1_rdy, TC * b + t + 1)
                sp.dma_start(row(x1_rows, TC * b + t), x_res[:, t % 2]).then_inc(st_x1[t % 2], 16)

            def z2(b, t):
                if t < 2:
                    load_res(b, t + 2)

            def zt(b, t):
                sp.wait_ge(z_hi, TC * b + t + 1)
                sp.wait_ge(z_lo, TC * b + t + 1)
                sp.dma_start(row(x1t_dram, TC * b + t), x1t_st[:, t % 2]).then_inc(st_x1t[t % 2], 16)

            first_half(sp, {"XL": load_x, "XT": xt, "AW": attention_weights, "WN": load_w13, "W2N": load_w2,
                            "RL": load_res, "YN": yn, "Z2": z2, "ZT": zt})

            for b in range(B):
                if b == 0:
                    sp.wait_ge(g_mm, B * KC)
                if b == B - 1:
                    sp.wait_ge(y_mm, B * TC)
                for slot in range(2):
                    sp.wait_ge(st_x1t[slot], 16 * slot_uses(b + 1, 0))
                sp.dma_start(x2t[:, b].rearrange("p t s k n -> p t (s k n)"),
                             x1t_dram[TC * b:TC * (b + 1)].rearrange("t p s k n -> p t (s k n)")
                             ).then_inc(ld_x2t[b], 16)
            sp.wait_ge(z_mm, B * TC)
            sp.wait_ge(z_lo, B * TC)
            for slot in range(2):
                sp.wait_ge(st_x1[slot], 16 * slot_uses(B, 0))

            def load_x1(b):
                sp.dma_start(x1r[:], x1_rows[bass.ds(TC * b, TC)].rearrange("t p d -> p t d")).then_inc(ld_x1r, 16)

            def store_out(b):
                for t in range(TC):
                    sp.wait_ge(out_rdy, TC * b + t + 1)
                    sp.dma_start(row(out_rows, TC * b + t), yv[:, t]).then_inc(st_out, 16)

            load_x1(0)
            with sp.Fori(0, B - 1) as b:
                store_out(b)
                sp.wait_ge(st_out, 16 * TC * (b + 1))
                load_x1(b + 1)
            store_out(B - 1)
            sp.wait_ge(st_out, 16 * B * TC)

        @block.tensor
        def _(pe):
            def three_passes(dst, a_hi, a_lo, b_hi, b_lo, start, stop):
                pe.matmul(dst, a_hi, b_hi, start=start, stop=False)
                pe.matmul(dst, a_hi, b_lo, start=False, stop=False)
                return pe.matmul(dst, a_lo, b_hi, start=False, stop=stop)

            def wait_small_bank(kind, b, t):
                key = (kind, traced(b), t)
                if key not in before:
                    return
                k, pb, pt = before[key]
                m = b + (pb - traced(b))
                if k == "XT":
                    pe.wait_ge(xt_lo, TC * m + pt + 1)
                elif k == "WT":
                    pe.wait_ge(wt_lo, 2 * HQ * m + pt + 1)
                elif k == "W2T":
                    pe.wait_ge(w2t_ev, 4 * m + pt + 1)
                elif k == "H2":
                    pe.wait_ge(h2_lo, 4 * m + pt + 1)
                elif k == "ZT":
                    pe.wait_ge(z_lo, TC * m + pt + 1)

            def transpose_tile(dst, tile):
                for k in range(KC):
                    last = pe.transpose(dst[:, k * P:(k + 1) * P], tile[:, k * P:(k + 1) * P], ident[:])
                return last

            def xt(b, t):
                if first(b) and t == 0:
                    pe.wait_ge(ld_eye, 16)
                wait_small_bank("XT", b, t)
                pe.wait_ge(x_norm, TC * b + t + 1)
                transpose_tile(bank("XT", b, t), x_in[:, t % 2]).then_inc(xt_mm, 1)

            def attention_weights(b, w):
                tiles = (w2a[:].rearrange("p (c d) -> p c d", c=KC), w2b[:].rearrange("p (c d) -> p c d", c=KC),
                         zn, w2a[:].rearrange("p (c d) -> p c d", c=KC))[w]
                for c in range(KC):
                    u = KC * w + c
                    if u >= 6:
                        pe.wait_ge(aw_lo, u - 5)
                    pe.wait_ge(aw_scale, u + 1)
                    transpose_tile(ps[u % 6], tiles[:, c]).then_inc(aw_mm, 1)

            def project(b, c, dst, w_t, done):
                if not isinstance(c, int):
                    raise ValueError
                for k in range(KC):
                    last = three_passes(dst[:], w_t[:, 0, k, c * P:(c + 1) * P], w_t[:, 1, k, c * P:(c + 1) * P],
                                        xnt[:, 0, k, :], xnt[:, 1, k, :], k == 0, k == KC - 1)
                last.then_inc(done, 1)

            def f(b, c):
                if c == 0:
                    pe.wait_ge(xt_hi, TC * (b + 1))
                    pe.wait_ge(xt_lo, TC * (b + 1))
                if first(b):
                    pe.wait_ge(aw_lo, 4 * KC)
                if c >= 2:
                    pe.wait_ge(gate_rdy, KC * b + c - 1)
                elif not first(b):
                    pe.wait_ge(y_norm, TC * b + (-3, 0)[c])
                project(b, c, ps[3 * (c % 2)], wft, f_mm)

            def i(b, c):
                if c >= 2:
                    pe.wait_ge(sli_rdy, KC * b + c - 1)
                elif c == 1 and not first(b):
                    pe.wait_ge(sli_rdy, KC * b)
                elif not first(b):
                    pe.wait_ge(y_norm, TC * b - 2)
                project(b, c, ps[3 * (c % 2) + 1], wit, i_mm)

            def g(b, c):
                if c >= 2:
                    pe.wait_ge(gs_rdy, KC * b + c - 1)
                elif c == 1 and not first(b):
                    pe.wait_ge(e_rdy, b)
                elif not first(b):
                    pe.wait_ge(y_norm, TC * b - 1)
                project(b, c, ps[3 * (c % 2) + 2], wgt, g_mm)

            def ms(b, t):
                pe.wait_ge(oadd, (KC - 1) * (b + 1))
                pe.wait_ge(gs_rdy, KC * (b + 1))
                pe.wait_ge(ones_set, 1)
                for tt in range(TC):
                    last = pe.matmul(ps[5][:, tt:tt + 1], osum[:, tt * P:(tt + 1) * P], ones[:, 0:1],
                                     start=True, stop=True)
                last.then_inc(ms_mm, 1)

            def y(b, t):
                if t == 0:
                    pe.wait_ge(aw_lo, 4 * KC)
                    pe.wait_ge(o_hi, KC * (b + 1))
                    pe.wait_ge(o_lo, KC * (b + 1))
                pe.wait_ge((gate_rdy, sli_rdy, gs_rdy, gate_rdy)[t], KC * b + (3, 3, 3, 4)[t])
                for k in range(KC):
                    last = three_passes(ps[t][:], ot[:, 0, k, t * P:(t + 1) * P], ot[:, 1, k, t * P:(t + 1) * P],
                                        wot[:, 0, k, :], wot[:, 1, k, :], k == 0, k == KC - 1)
                last.then_inc(y_mm, 1)

            def zt(b, t):
                wait_small_bank("ZT", b, t)
                pe.wait_ge(z_norm, TC * b + t + 1)
                transpose_tile(bank("ZT", b, t), zn[:, t]).then_inc(z_mm, 1)

            def wt(b, t):
                wait_small_bank("WT", b, t)
                pe.wait_ge(w_scaled, 2 * HQ * b + t + 1)
                transpose_tile(bank("WT", b, t), w_in[:, t % 2]).then_inc(wt_mm, 1)

            def w2t_(b, t):
                wait_small_bank("W2T", b, t)
                pe.wait_ge(w2_fly, 8 * (b + 1))
                transpose_tile(bank("W2T", b, t), w2a[:, t * 512:(t + 1) * 512]).then_inc(w2t_mm, 1)

            def h2(b, t):
                if t == 0:
                    pe.wait_ge(ld_had, 16)
                wait_small_bank("H2", b, t)
                pe.wait_ge(w2t_ev, 4 * b + t + 1)
                pe.matmul(bank("H2", b, t)[:], had[:], w2b[:, t * 512:(t + 1) * 512], start=True, stop=True
                          ).then_inc(h2_mm, 1)

            first_half(pe, {"XT": xt, "AW": attention_weights, "AO": lambda b, t: attention_weights(b, 3),
                            "F": f, "I": i, "G": g, "MS": ms, "Y": y, "ZT": zt, "WT": wt, "W2T": w2t_, "H2": h2})

            def gate_up(b, c, s):
                n = HC * b + c
                for w_t, dst, free, done in ((w1t, ps[4 + s], sil_rdy, ga_mm), (w3t, ps[6 + s], hid_rdy, up_mm)):
                    if not (isinstance(n, int) and n < 2):
                        pe.wait_ge(free, passed(n, c))
                    for k in range(KC):
                        xs = [x2t[:, bass.ds(b, 1), :, h, k, :].squeeze(1) for h in range(2)]
                        ws = [w_t[:, h, k, bass.ds(c * P, P)] for h in range(2)]
                        last = three_passes(dst[:], ws[0], ws[1], xs[0], xs[1], k == 0, k == KC - 1)
                    last.then_inc(done, 1)

            def down(b, c, s, start=False, stop=False):
                n = HC * b + c
                pe.wait_ge(hid_hi, n + 1)
                pe.wait_ge(hid_lo, n + 1)
                for t in range(TC):
                    if start:
                        pe.wait_ge(y_free, TC * b + 1)
                    w_hi, w_lo = (w2t[:, h, bass.ds(c, 1), :].squeeze(1) for h in range(2))
                    last = three_passes(ps[t][:], hsp[:, s, 0, t * P:(t + 1) * P], hsp[:, s, 1, t * P:(t + 1) * P],
                                        w_hi, w_lo, start, stop)
                last.then_inc(d_mm, 1)

            def batch_row(b, last):
                gate_up(b, 1, 1)
                down(b, 0, 0, start=True)
                with pe.Fori(0, HC // 2 - 1) as j:
                    c = 2 * j + 1
                    gate_up(b, c + 1, 0)
                    down(b, c, 1)
                    gate_up(b, c + 2, 1)
                    down(b, c + 1, 0)
                if not last:
                    gate_up(b + 1, 0, 0)
                down(b, HC - 1, 1, stop=True)

            pe.wait_ge(z_hi, B * TC)
            pe.wait_ge(z_lo, B * TC)
            pe.wait_ge(wt_lo, 2 * HC)
            pe.wait_ge(h2_lo, HC)
            pe.wait_ge(e_rdy, B)
            pe.wait_ge(sli_rdy, B * KC)
            pe.wait_ge(ld_x2t[0], 16)
            gate_up(0, 0, 0)
            pe.wait_ge(diag_rdy, B)
            for q in range(B):
                last = pe.matmul(ps[3][:, q * P:(q + 1) * P], ones[:], diag[:, q], start=True, stop=True)
            last.then_inc(row_mm, 1)
            for b in range(1, B):
                pe.wait_ge(ld_x2t[b], 16)
            with pe.Fori(0, B - 1) as b:
                batch_row(b, False)
            batch_row(B - 1, True)

        @block.scalar
        def _(act):
            def xt(b, t):
                act.wait_ge(xt_mm, TC * b + t + 1)
                act.activation(xnt[:, 0, :, t * P:(t + 1) * P], quarters(bank("XT", b, t)), ACT.Copy).then_inc(xt_hi, 1)

            def attention_weights(b, w):
                src = (w2a[:].rearrange("p (c d) -> p c d", c=KC), w2b[:].rearrange("p (c d) -> p c d", c=KC),
                       zn, w2a[:].rearrange("p (c d) -> p c d", c=KC))[w]
                act.wait_ge(ld_aw[w], 16)
                for c in range(KC):
                    act.wait_ge(aw_sq, KC * w + c)
                    act.activation(osq[:], src[:, c], ACT.Square, accum_out=norm2[:, w, c:c + 1]).then_inc(aw_sq, 1)
                for c in range(KC):
                    u = KC * w + c
                    act.wait_ge(aw_mm, u + 1)
                    act.activation((wft, wit, wgt, wot)[w][:, 0, :, c * P:(c + 1) * P], quarters(ps[u % 6]),
                                   ACT.Copy).then_inc(aw_hi, 1)

            def f(b, c):
                n = KC * b + c
                if first(b) and c == 0:
                    act.wait_ge(unscale_rdy, 3)
                act.wait_ge(f_mm, n + 1)
                if not (first(b) and c == 0):
                    act.wait_ge(o_rdy, n)
                act.activation(gate[:], ps[3 * (c % 2)][:], ACT.Sigmoid, scale=unscale[:, 0, c:c + 1]
                               ).then_inc(gate_rdy, 1)

            def i(b, c):
                n = KC * b + c
                act.wait_ge(i_mm, n + 1)
                act.wait_ge(sli_rdy, n)
                act.activation(sg[:, 0], ps[3 * (c % 2) + 1][:], ACT.Sigmoid, scale=unscale[:, 1, c:c + 1]
                               ).then_inc(sgi_rdy, 1)

            def g(b, c):
                n = KC * b + c
                act.wait_ge(g_mm, n + 1)
                act.wait_ge(gs_rdy, n)
                act.activation(sg[:, 1], ps[3 * (c % 2) + 2][:], ACT.Sigmoid, scale=unscale[:, 2, c:c + 1]
                               ).then_inc(sgg_rdy, 1)

            def o(b, c):
                n = KC * b + c
                act.wait_ge(o_rdy, n + 1)
                if c == 0:
                    act.wait_ge(ms_mm, b)
                else:
                    act.wait_ge(oadd, (KC - 1) * b + c - 1)
                act.activation(osum[:] if c == 0 else osq[:], o_s[:, c % 2], ACT.Square).then_inc(osq_rdy, 1)
                act.wait_ge(op_rdy, n + 1)
                act.activation(ot[:, 0, c, :], gs[:, c % 2], ACT.Copy).then_inc(o_hi, 1)

            def yn(b, t):
                act.wait_ge(y_ab, TC * b + t + 1)
                act.activation(zn[:, t], ps[t][:], ACT.Identity, bias=ab[:, t, 1:2], scale=ab[:, t, 0:1]
                               ).then_inc(y_norm, 1)

            def zt(b, t):
                act.wait_ge(z_mm, TC * b + t + 1)
                if t < 2:
                    act.wait_ge(ld_res[t % 2], 16 * (slot_uses(b, t) + 1))
                else:
                    act.wait_ge(st_x1t[t % 2], 16 * slot_uses(b, t))
                act.activation(x1t_st[:, t % 2, 0], quarters(bank("ZT", b, t)), ACT.Copy).then_inc(z_hi, 1)

            def wn(b, t):
                m = HQ * b + t
                act.wait_ge(ld_w13, 32 * (m + 1))
                act.wait_ge(w_srdy, m)
                for w in range(2):
                    act.wait_ge(w_sq, 2 * m + w)
                    act.activation(w_junk, w_in[:, w], ACT.Square, accum_out=wn2[:, w:w + 1]).then_inc(w_sq, 1)

            def wt(b, t):
                act.wait_ge(wt_mm, 2 * HQ * b + t + 1)
                act.activation((w1t, w3t)[t % 2][:, 0, :, bass.ds((HQ * b + t // 2) * P, P)], quarters(bank("WT", b, t)),
                               ACT.Copy).then_inc(wt_hi, 1)

            def w2n(b, t):
                act.wait_ge(ld_w2, 16 * (b + 1))
                act.wait_ge(w2_scaled, b)
                if not first(b):
                    act.wait_ge(h2_mm, 4 * b)
                act.activation(w2b[:], w2a[:], ACT.Square, accum_out=w2n2[:]).then_inc(w2_sq, 1)

            def w2t_(b, t):
                act.wait_ge(w2t_mm, 4 * b + t + 1)
                act.activation(w2b[:, t * 512:(t + 1) * 512], bank("W2T", b, t)[:], ACT.Copy).then_inc(w2t_ev, 1)

            def h2(b, t):
                act.wait_ge(h2_mm, 4 * b + t + 1)
                act.activation(w2t[:, 0, 4 * t:4 * t + 4, bass.ds(b * P, P)], quarters(bank("H2", b, t)), ACT.Copy
                               ).then_inc(h2_hi, 1)

            first_half(act, {"XT": xt, "AW": attention_weights, "AO": lambda b, t: attention_weights(b, 3),
                             "F": f, "I": i, "G": g, "O": o, "YN": yn, "ZT": zt, "WN": wn, "WT": wt,
                             "W2N": w2n, "W2T": w2t_, "H2": h2})

            def gate_up(b, c, s):
                n = HC * b + c
                act.wait_ge(ga_mm, n + 1)
                if not (isinstance(n, int) and n < 2):
                    act.wait_ge(sil_rdy, passed(n, c))
                act.activation(sga[:, s], ps[4 + s][:], ACT.Sigmoid, scale=gate_c[:, bass.ds(c, 1)]
                               ).then_inc(sga_rdy, 1)
                act.wait_ge(hid_rdy, n + 1)
                if not (isinstance(n, int) and n < 2):
                    act.wait_ge(d_mm, passed(n, c))
                act.activation(hsp[:, s, 0], hd[:, s], ACT.Copy).then_inc(hid_hi, 1)

            def norm_out(b):
                act.wait_ge(v_ab, b + 1)
                for t in range(TC):
                    act.activation(yv[:, t], yv[:, t], ACT.Identity, bias=ab[:, t, 1:2],
                                   scale=rstd[:, 1, t:t + 1]).then_inc(v_norm, 1)

            def batch_row(b, last):
                gate_up(b, 1, 1)
                with act.Fori(0, HC // 2 - 1) as j:
                    c = 2 * j + 1
                    gate_up(b, c + 1, 0)
                    gate_up(b, c + 2, 1)
                if not last:
                    gate_up(b + 1, 0, 0)
                norm_out(b)

            act.wait_ge(hid_scale, 2)
            act.wait_ge(z_lo, B * TC)
            act.wait_ge(o_lo, B * KC)
            act.wait_ge(x1_rdy, B * TC)
            for slot in range(2):
                act.wait_ge(st_x1t[slot], 16 * slot_uses(B, 0))
                act.wait_ge(st_x1[slot], 16 * slot_uses(B, 0))
            gate_up(0, 0, 0)
            with act.Fori(0, B - 1) as b:
                batch_row(b, False)
            batch_row(B - 1, True)

        @block.vector
        def _(dve):
            dve.memset(ones[:], 1.0).then_inc(ones_set, 1)
            dve.memset(neg_half[:], -0.5).then_inc(half_set, 1)

            def exponent_scales(sem_, base, norm, exp, s, inv, done, done_at):
                dve.tensor_scalar(exp.bitcast(I32), norm.bitcast(I32), 24, None, ALU.logical_shift_right
                                  ).then_inc(sem_, 1)
                dve.wait_ge(sem_, base + 1)
                dve.tensor_scalar(exp.bitcast(I32), exp.bitcast(I32), float(F_LEAST), None, ALU.max
                                  ).then_inc(sem_, 1)
                dve.wait_ge(sem_, base + 2)
                dve.tensor_scalar(inv.bitcast(I32), exp.bitcast(I32), BIT, (127 - ROW_EXP) * BIT, ALU.mult, ALU.add
                                  ).then_inc(sem_, 1)
                dve.tensor_scalar(s.bitcast(I32), exp.bitcast(I32), -BIT, (127 + ROW_EXP) * BIT, ALU.mult, ALU.add
                                  ).then_inc(done, 1)
                dve.wait_ge(done, done_at)

            def row_stats(sem_, base, src, which, t):
                dve.bn_stats(st[:, which], src).then_inc(sem_, 1)
                dve.drain()
                dve.bn_aggr(mv[:, which, t], st[:, which]).then_inc(sem_, 1)
                dve.wait_ge(sem_, base + 2)

            def x1(b, t):
                m = TC * b + t
                dve.wait_ge(ld_x[t % 2], 16 * (slot_uses(b, t) + 1))
                row_stats(x_chain, 2 * m, x_in[:, t % 2], 0, t)
                dve.tensor_scalar(var[:, 0, t:t + 1], mv[:, 0, t, 1:2], EPS, 2.0 ** (-2 * X_EXP), ALU.add, ALU.mult
                                  ).then_inc(x_var, 1)

            def x2(b, t):
                m = TC * b + t
                dve.wait_ge(x_rstd, m + 1)
                dve.tensor_scalar(x_in[:, t % 2], x_in[:, t % 2], mv[:, 0, t, 0:1], rstd[:, 0, t:t + 1],
                                  ALU.subtract, ALU.mult).then_inc(x_norm, 1)

            def xt(b, t):
                dve.wait_ge(xt_hi, TC * b + t + 1)
                dve.tensor_tensor(xnt[:, 1, :, t * P:(t + 1) * P], quarters(bank("XT", b, t)),
                                  xnt[:, 0, :, t * P:(t + 1) * P], ALU.subtract).then_inc(xt_lo, 1)

            def split_attention_weights(w):
                for c in range(KC):
                    u = KC * w + c
                    w_t = (wft, wit, wgt, wot)[w]
                    dve.wait_ge(aw_hi, u + 1)
                    dve.tensor_tensor(w_t[:, 1, :, c * P:(c + 1) * P], quarters(ps[u % 6]),
                                      w_t[:, 0, :, c * P:(c + 1) * P], ALU.subtract).then_inc(aw_lo, 1)

            def attention_weights(b, w):
                src = (w2a[:].rearrange("p (c d) -> p c d", c=KC), w2b[:].rearrange("p (c d) -> p c d", c=KC), zn)[w]
                dve.wait_ge(aw_sq, KC * (w + 1))
                exponent_scales(aw_chain, 3 * w, norm2[:, w], s_tmp[:, 0:KC], row_s[:, w], row_inv[:, w],
                                aw_srdy, w + 1)
                for c in range(KC):
                    dve.tensor_scalar(src[:, c], src[:, c], row_s[:, w, c:c + 1], None, ALU.mult).then_inc(aw_scale, 1)
                dve.tensor_scalar(unscale[:, w], row_inv[:, w], 2.0 ** -X_EXP, None, ALU.mult).then_inc(unscale_rdy, 1)
                split_attention_weights(w)

            def output_weights(b, t):
                w, src = 3, w2a[:].rearrange("p (c d) -> p c d", c=KC)
                dve.wait_ge(aw_sq, 4 * KC)
                dve.tensor_reduce(s_tmp[:, 4:5], norm2[:, w], AX.X, ALU.max).then_inc(part_max, 1)
                dve.wait_ge(ld_gw, 16)
                dve.tensor_tensor(g_coef[:], row_inv[:, 1], row_inv[:, 2], ALU.mult).then_inc(coef_chain, 1)
                dve.wait_ge(coef_chain, 1)
                dve.tensor_tensor(g_coef[:], g_coef[:], gw[:], ALU.mult).then_inc(coef_chain, 1)
                dve.wait_ge(coef_chain, 2)
                dve.tensor_scalar(g_coef[:].bitcast(I32), g_coef[:].bitcast(I32), 0x7FFFFFFF, None, ALU.bitwise_and).then_inc(coef_chain, 1)
                dve.wait_ge(coef_chain, 3)
                dve.tensor_reduce(s_tmp[:, 5:6], g_coef[:], AX.X, ALU.max).then_inc(part_max, 1)
                dve.wait_ge(all_max, 1)
                exponent_scales(aw_chain, 9, s_tmp[:, 6:7], s_tmp[:, 0:1], row_s[:, w, 0:1], row_inv[:, w, 0:1],
                                aw_srdy, 4)
                for c in range(KC):
                    dve.tensor_scalar(src[:, c], src[:, c], row_s[:, w, 0:1], None, ALU.mult).then_inc(aw_scale, 1)
                o_exp = 126 - NORM_BOUND_EXP + HID_EXP
                dve.wait_ge(all_max, 2)
                dve.tensor_scalar(s_tmp[:, 1:2].bitcast(I32), s_tmp[:, 7:8].bitcast(I32), 23, None,
                                  ALU.logical_shift_right).then_inc(coef_chain, 1)
                dve.wait_ge(coef_chain, 4)
                dve.tensor_scalar(s_tmp[:, 2:3].bitcast(I32), s_tmp[:, 1:2].bitcast(I32), -BIT, (127 + o_exp) * BIT,
                                  ALU.mult, ALU.add).then_inc(coef_chain, 1)
                dve.tensor_scalar(s_tmp[:, 3:4].bitcast(I32), s_tmp[:, 1:2].bitcast(I32), BIT, (127 - o_exp) * BIT,
                                  ALU.mult, ALU.add).then_inc(coef_chain, 1)
                dve.wait_ge(coef_chain, 6)
                dve.scalar_tensor_tensor(g_coef[:], gw[:], s_tmp[:, 2:3], unscale[:, 2], ALU.mult, ALU.mult
                                         ).then_inc(coef_chain, 1)
                dve.wait_ge(coef_chain, 7)
                dve.tensor_scalar(g_coef[:], g_coef[:], -1.0, None, ALU.mult).then_inc(coef_rdy, 1)
                dve.tensor_tensor(y_inv[:, 0:1], s_tmp[:, 3:4], row_inv[:, w, 0:1], ALU.mult).then_inc(coef_chain, 1)
                dve.wait_ge(coef_chain, 8)
                dve.tensor_tensor(y_inv[:, 1:2], y_inv[:, 0:1], y_inv[:, 0:1], ALU.mult).then_inc(yinv_rdy, 1)
                dve.wait_ge(coef_rdy, 1)
                dve.wait_ge(yinv_rdy, 1)
                split_attention_weights(w)

            def i(b, c):
                n = KC * b + c
                dve.wait_ge(sgi_rdy, n + 1)
                dve.scalar_tensor_tensor(sl[:], ps[3 * (c % 2) + 1][:], unscale[:, 1, c:c + 1], sg[:, 0],
                                         ALU.mult, ALU.mult).then_inc(sli_rdy, 1)
                dve.wait_ge(sli_rdy, n + 1)
                dve.wait_ge(gate_rdy, n + 1)
                dve.scalar_tensor_tensor(sl[:], gate[:], 1.0, sl[:], ALU.subtract, ALU.mult
                                         ).then_inc(nv_rdy, 1)
                dve.wait_ge(nv_rdy, n + 1)
                if not (first(b) and c < 2):
                    dve.wait_ge(osq_rdy, n - 1)
                dve.tensor_tensor_scan(o_s[:, c % 2], gate[:], sl[:], 0.0, ALU.mult, ALU.add
                                       ).then_inc(o_rdy, 1)

            def g(b, c):
                n = KC * b + c
                dve.wait_ge(sgg_rdy, n + 1)
                if not (first(b) and c < 2):
                    dve.wait_ge(o_lo, n - 1)
                dve.scalar_tensor_tensor(gs[:, c % 2], ps[3 * (c % 2) + 2][:], g_coef[:, c:c + 1], sg[:, 1],
                                         ALU.mult, ALU.mult).then_inc(gs_rdy, 1)
                dve.wait_ge(gs_rdy, n + 1)
                dve.wait_ge(o_rdy, n + 1)
                dve.tensor_tensor(gs[:, c % 2], gs[:, c % 2], o_s[:, c % 2], ALU.mult).then_inc(op_rdy, 1)

            def ms(b, t):
                dve.wait_ge(ms_mm, b + 1)
                dve.tensor_scalar(ms_eps[:], ps[5][:, 0:TC], EPS / D, EPS * EPS, ALU.mult, ALU.add).then_inc(e_rdy, 1)
                dve.wait_ge(e_rdy, b + 1)

            def y(b, t):
                m = TC * b + t
                dve.wait_ge(y_mm, m + 1)
                row_stats(y_chain, 2 * m, ps[t][:], 1, t)
                dve.scalar_tensor_tensor(var[:, 1, t:t + 1], mv[:, 1, t, 1:2], y_inv[:, 1:2], ms_eps[:, t:t + 1],
                                         ALU.mult, ALU.add).then_inc(y_var, 1)

            def yn(b, t):
                m = TC * b + t
                dve.wait_ge(y_rstd, m + 1)
                dve.tensor_scalar(ab[:, t, 0:1], rstd[:, 1, t:t + 1], y_inv[:, 0:1], None, ALU.mult
                                  ).then_inc(y_scale, 1)
                dve.wait_ge(y_scale, m + 1)
                dve.scalar_tensor_tensor(ab[:, t, 1:2], mv[:, 1, t, 0:1], -1.0, ab[:, t, 0:1], ALU.mult, ALU.mult
                                         ).then_inc(y_ab, 1)

            def z1(b, t):
                m = TC * b + t
                dve.wait_ge(x1_rdy, m + 1)
                row_stats(z_chain, 2 * m, x_res[:, t % 2], 2, t)
                dve.tensor_scalar(var[:, 2, t:t + 1], mv[:, 2, t, 1:2], EPS, 2.0 ** (-2 * X_EXP), ALU.add, ALU.mult
                                  ).then_inc(z_var, 1)

            def z2(b, t):
                m = TC * b + t
                dve.wait_ge(z_rstd, m + 1)
                dve.tensor_scalar(zn[:, t], x_res[:, t % 2], mv[:, 2, t, 0:1], rstd[:, 2, t:t + 1],
                                  ALU.subtract, ALU.mult).then_inc(z_norm, 1)

            def zt(b, t):
                dve.wait_ge(z_hi, TC * b + t + 1)
                dve.tensor_tensor(x1t_st[:, t % 2, 1], quarters(bank("ZT", b, t)), x1t_st[:, t % 2, 0], ALU.subtract
                                  ).then_inc(z_lo, 1)

            def wn(b, t):
                m = HQ * b + t
                dve.wait_ge(w_sq, 2 * (m + 1))
                dve.wait_ge(w_scaled, 2 * m)
                exponent_scales(w_chain, 3 * m, wn2[:], wexp[:], w_s[:],
                                w13_inv[:, :, bass.ds(m, 1)].squeeze(2), w_srdy, m + 1)

            def wt(b, t):
                c = HQ * b + t // 2
                w_t = (w1t, w3t)[t % 2]
                dve.wait_ge(wt_hi, 2 * HQ * b + t + 1)
                dve.tensor_tensor(w_t[:, 1, :, bass.ds(c * P, P)], quarters(bank("WT", b, t)),
                                  w_t[:, 0, :, bass.ds(c * P, P)], ALU.subtract).then_inc(wt_lo, 1)

            def w2n(b, t):
                dve.wait_ge(w2_sq, b + 1)
                exponent_scales(w2_chain, 3 * b, w2n2[:], w2exp[:], w2_s[:], w2_inv[:, bass.ds(b, 1)], w2_srdy, b + 1)
                dve.tensor_scalar(w2a[:], w2a[:], w2_s[:], 2.0 ** -5, ALU.mult, ALU.mult).then_inc(w2_scaled, 1)

            def h2(b, t):
                dve.wait_ge(h2_hi, 4 * b + t + 1)
                dst = w2t[:, :, 4 * t:4 * t + 4, bass.ds(b * P, P)]
                dve.tensor_tensor(dst[:, 1], quarters(bank("H2", b, t)), dst[:, 0], ALU.subtract).then_inc(h2_lo, 1)

            first_half(dve, {"X1": x1, "X2": x2, "XT": xt, "AW": attention_weights, "AO": output_weights,
                             "I": i, "G": g, "MS": ms, "Y": y, "YN": yn, "Z1": z1, "Z2": z2, "ZT": zt,
                             "WN": wn, "WT": wt, "W2N": w2n, "H2": h2})

            dve.tensor_tensor(up_c[:], w13_inv[:, 0], w13_inv[:, 1], ALU.mult).then_inc(h_chain, 1)
            dve.wait_ge(h_chain, 1)
            dve.tensor_reduce(hid_s[:, 0:1], up_c[:], AX.X, ALU.max).then_inc(hid_part, 1)
            dve.wait_ge(hid_max, 1)
            dve.tensor_scalar(hid_s[:, 2:3].bitcast(I32), hid_s[:, 1:2].bitcast(I32), -1.0,
                              (2 * 127 - NORM_BOUND_EXP + HID_EXP) * BIT, ALU.mult, ALU.add).then_inc(h_chain, 1)
            dve.wait_ge(h_chain, 2)
            dve.tensor_scalar(up_c[:], w13_inv[:, 1], hid_s[:, 2:3], 2.0 ** -X_EXP, ALU.mult, ALU.mult
                              ).then_inc(hid_scale, 1)
            dve.tensor_scalar(gate_c[:], w13_inv[:, 0], 2.0 ** -X_EXP, None, ALU.mult).then_inc(hid_scale, 1)
            dve.wait_ge(o_lo, B * KC)
            dve.wait_ge(x1_rdy, B * TC)
            dve.wait_ge(z_mm, B * TC)
            for slot in range(2):
                dve.wait_ge(st_x1[slot], 16 * slot_uses(B, 0))
                dve.wait_ge(st_x1t[slot], 16 * slot_uses(B, 0))
            for q in range(B):
                dve.tensor_scalar(diag[:, q], ident[:], w2_inv[:, q:q + 1], None, ALU.mult).then_inc(diag_rdy, 1)

            def gate_up(b, c, s):
                n = HC * b + c
                dve.wait_ge(sga_rdy, n + 1)
                dve.scalar_tensor_tensor(sil[:, s], ps[4 + s][:], gate_c[:, bass.ds(c, 1)], sga[:, s],
                                         ALU.mult, ALU.mult).then_inc(sil_rdy, 1)
                dve.wait_ge(sil_rdy, n + 1)
                dve.wait_ge(up_mm, n + 1)
                if not (isinstance(n, int) and n < 2):
                    dve.wait_ge(hid_lo, passed(n, c))
                dve.scalar_tensor_tensor(hd[:, s], ps[6 + s][:], up_c[:, bass.ds(c, 1)], sil[:, s],
                                         ALU.mult, ALU.mult).then_inc(hid_rdy, 1)

            def norm_out(b):
                dve.wait_ge(d_mm, HC * (b + 1))
                dve.wait_ge(ld_x1r, 16 * (b + 1))
                for t in range(TC):
                    dve.tensor_tensor(yv[:, t], ps[t][:], row_c[:], ALU.mult).then_inc(y_free, 1)
                for t in range(TC):
                    dve.wait_ge(y_free, TC * b + t + 2)
                    row_stats(v_chain, 2 * (TC * b + t), yv[:, t], 1, t)
                dve.tensor_scalar(var[:, 1], mv[:, 1, :, 1], EPS, None, ALU.add).then_inc(v_var, 1)
                dve.wait_ge(v_rstd, b + 1)
                dve.scalar_tensor_tensor(ab[:, :, 1], mv[:, 1, :, 0], -1.0, rstd[:, 1], ALU.mult, ALU.mult
                                         ).then_inc(v_ab, 1)

            def batch_row(b, last):
                gate_up(b, 1, 1)
                with dve.Fori(0, HC // 2 - 1) as j:
                    c = 2 * j + 1
                    gate_up(b, c + 1, 0)
                    gate_up(b, c + 2, 1)
                if not last:
                    gate_up(b + 1, 0, 0)
                norm_out(b)

            dve.wait_ge(hid_scale, 2)
            gate_up(0, 0, 0)
            dve.wait_ge(row_mm, 1)
            dve.tensor_scalar(row_c[:], ps[3][:], hid_s[:, 1:2],
                              2.0 ** (NORM_BOUND_EXP - HID_EXP + 5) * float(np.float32(1.0 / np.sqrt(H))),
                              ALU.mult, ALU.mult).then_inc(y_free, 1)
            dve.wait_ge(y_free, 1)
            with dve.Fori(0, B - 1) as b:
                batch_row(b, False)
            batch_row(B - 1, True)

        @block.gpsimd
        def _(pool):
            def rsqrt(dst, src, done):
                pool.tensor_tensor(dst, src, neg_half[:].broadcast_to(src.shape), ALU.pow).then_inc(done, 1)

            def x1(b, t):
                pool.wait_ge(x_var, TC * b + t + 1)
                if first(b) and t == 0:
                    pool.wait_ge(half_set, 1)
                rsqrt(rstd[:, 0, t:t + 1], var[:, 0, t:t + 1], x_rstd)

            def output_weights(b, t):
                for n in range(2):
                    pool.wait_ge(part_max, n + 1)
                    pool.partition_all_reduce(s_tmp[:, 6 + n:7 + n], s_tmp[:, 4 + n:5 + n], P, RMAX
                                              ).then_inc(all_max, 1)

            def o(b, c):
                n = KC * b + c
                if c > 0:
                    pool.wait_ge(osq_rdy, n + 1)
                    pool.wait_ge(oadd, (KC - 1) * b + c - 1)
                    pool.tensor_tensor(osum[:], osum[:], osq[:], ALU.add).then_inc(oadd, 1)
                pool.wait_ge(o_hi, n + 1)
                pool.tensor_tensor(ot[:, 1, c, :], gs[:, c % 2], ot[:, 0, c, :], ALU.subtract).then_inc(o_lo, 1)

            def y(b, t):
                pool.wait_ge(y_var, TC * b + t + 1)
                rsqrt(rstd[:, 1, t:t + 1], var[:, 1, t:t + 1], y_rstd)

            def yn(b, t):
                pool.wait_ge(y_norm, TC * b + t + 1)
                pool.wait_ge(ld_res[t % 2], 16 * (slot_uses(b, t) + 1))
                pool.tensor_tensor(x_res[:, t % 2], x_res[:, t % 2], zn[:, t], ALU.add).then_inc(x1_rdy, 1)

            def z1(b, t):
                pool.wait_ge(z_var, TC * b + t + 1)
                rsqrt(rstd[:, 2, t:t + 1], var[:, 2, t:t + 1], z_rstd)

            def wn(b, t):
                m = HQ * b + t
                pool.wait_ge(w_srdy, m + 1)
                for w in range(2):
                    pool.tensor_tensor(w_in[:, w], w_in[:, w], w_s[:, w:w + 1].broadcast_to((P, D)), ALU.mult).then_inc(w_scaled, 1)

            def fly(b, k):
                stage, half = k // 2, k % 2
                if k == 0:
                    pool.wait_ge(w2_scaled, b + 1)
                if half == 0:
                    pool.wait_ge(w2_fly, 8 * b + k)
                src, dst = (w2a, w2b) if stage % 2 == 0 else (w2b, w2a)
                s, d = (v[:].rearrange("p (g two w) -> p g two w", two=2, w=P << stage) for v in (src, dst))
                pool.tensor_tensor(d[:, :, half], s[:, :, 0], s[:, :, 1], ALU.subtract if half else ALU.add
                                   ).then_inc(w2_fly, 1)

            first_half(pool, {"X1": x1, "AO": output_weights, "O": o, "Y": y, "YN": yn, "Z1": z1, "WN": wn,
                              "FW": fly})

            pool.wait_ge(hid_part, 1)
            pool.partition_all_reduce(hid_s[:, 1:2], hid_s[:, 0:1], P, RMAX).then_inc(hid_max, 1)

            def split(b, c, s):
                n = HC * b + c
                pool.wait_ge(hid_hi, n + 1)
                pool.tensor_tensor(hsp[:, s, 1], hd[:, s], hsp[:, s, 0], ALU.subtract).then_inc(hid_lo, 1)

            def residual(b):
                pool.wait_ge(v_var, b + 1)
                rsqrt(rstd[:, 1], var[:, 1], v_rstd)
                pool.wait_ge(ld_x1r, 16 * (b + 1))
                for t in range(TC):
                    pool.wait_ge(v_norm, TC * b + t + 1)
                    pool.tensor_tensor(yv[:, t], yv[:, t], x1r[:, t], ALU.add).then_inc(out_rdy, 1)

            def batch_row(b, last):
                split(b, 1, 1)
                with pool.Fori(0, HC // 2 - 1) as j:
                    c = 2 * j + 1
                    split(b, c + 1, 0)
                    split(b, c + 2, 1)
                if not last:
                    split(b + 1, 0, 0)
                residual(b)

            split(0, 0, 0)
            with pool.Fori(0, B - 1) as b:
                batch_row(b, False)
            batch_row(B - 1, True)


_INS = ["L0_attn_hidden_states", "L0_attn_Wi", "L0_attn_Wf", "L0_attn_Wg", "L0_attn_Wo", "L0_attn_gnorm_w",
        "L0_ffn_W1", "L0_ffn_W2", "L0_ffn_W3"]


def kernel(**inputs):
    import concourse.bacc as bacc
    from concourse.bass_utils import run_bass_kernel_spmd

    nc = bacc.Bacc("TRN2", target_bir_lowering=False, num_devices=1)
    sign = np.ones((1, 1), np.float32)
    while sign.shape[0] < P:
        sign = np.block([[sign, sign], [sign, -sign]])
    arrays = {name: np.ascontiguousarray(inputs[name]) for name in _INS}
    arrays["gnorm"] = np.ascontiguousarray(arrays.pop("L0_attn_gnorm_w").reshape(-1, P).T)
    arrays["eye"] = np.eye(P, dtype=np.float32)
    arrays["hadamard"] = np.ascontiguousarray(sign)
    aps = {name: nc.dram_tensor(name, a.shape, mybir.dt.from_np(a.dtype), kind="ExternalInput").ap()
           for name, a in arrays.items()}
    out = nc.dram_tensor("out", arrays[_INS[0]].shape, F32, kind="ExternalOutput").ap()
    mixer_ffn_kernel(nc, aps["L0_attn_hidden_states"], aps["L0_attn_Wi"], aps["L0_attn_Wf"], aps["L0_attn_Wg"],
                     aps["L0_attn_Wo"], aps["gnorm"], aps["L0_ffn_W1"], aps["L0_ffn_W2"],
                     aps["L0_ffn_W3"], aps["eye"], aps["hadamard"], out)
    results = run_bass_kernel_spmd(nc, [arrays], core_ids=[0])
    return results.results[0]["out"]
```

```python
from contextlib import ExitStack

import numpy as np
import concourse.bass as bass
from concourse import mybir

ALU = mybir.AluOpType
ACT = mybir.ActivationFunctionType
AX = mybir.AxisListType
F32 = mybir.dt.float32
F16 = mybir.dt.float16
I32 = mybir.dt.int32
RMAX = bass.bass_isa.ReduceOp.max
RSUM = bass.bass_isa.ReduceOp.add

P = 128
UNIT_WIDTH = 64
EPS = 1e-5
X_EXP = 11
ROW_EXP = 77
F_LEAST = 24
BIT = float(1 << 23)
NORM_BOUND_EXP = 9 + 29
HID_EXP = 15


def mixer_ffn_kernel(nc, x, w_i, w_f, w_g, w_o, gnorm, w_1, w_3, w_1t, w_3t, w_2t, eye, hadamard, out):
    B, T, D = x.shape
    H = w_1.shape[0]
    KC = D // P
    TC = T // P
    HC = H // P
    HQ = HC // B
    assert T == D == 512 and KC == TC == B == 4 and HC == 16

    x_rows = x.rearrange("b (t p) d -> (b t) p d", p=P)
    out_rows = out.rearrange("b (t p) d -> (b t) p d", p=P)
    w1_rows = w_1.rearrange("(c p) d -> c p d", p=P)
    w3_rows = w_3.rearrange("(c p) d -> c p d", p=P)
    UNITS, UW = w_2t.shape[0], w_2t.shape[3]
    UB = UNITS // B
    x1_rows = nc.dram_tensor("x1_rows", (B * TC, P, D), F32, kind="Internal").ap()
    x1t_dram = nc.dram_tensor("x1t_split", (B * TC, P, 2, KC, P), F16, kind="Internal").ap()

    with ExitStack() as ctx:
        def sb(name, shape, dt=F32, c=ctx):
            return c.enter_context(nc.sbuf_tensor(name, shape, dt))

        def sem(name):
            return ctx.enter_context(nc.semaphore(name))

        ident = sb("ident", [P, P])
        had = sb("had", [P, P])
        ones = sb("ones", [P, 1])
        neg_half = sb("neg_half", [P, 1])
        gw = sb("gw", [P, KC])
        norm2 = sb("norm2", [P, 4, KC])
        row_s = sb("row_s", [P, 4, KC])
        row_inv = sb("row_inv", [P, 4, KC])
        unscale = sb("unscale", [P, 3, KC])
        g_coef = sb("g_coef", [P, KC])
        s_tmp = sb("s_tmp", [P, 8])
        y_inv = sb("y_inv", [P, 2])
        wn2 = sb("wn2", [P, 2])
        wn2_in = sb("wn2_in", [P, 2])
        wmax = sb("wmax", [P, 2])
        wexp = sb("wexp", [P, 2])
        w_s = sb("w_s", [P, 2])
        w13_inv = sb("w13_inv", [P, 2, HC])
        w2n2 = sb("w2n2", [P, 3])
        w2exp = sb("w2exp", [P, 1])
        w2_s = sb("w2_s", [P, 1])
        w2_inv = sb("w2_inv", [P, UNITS])
        gate_c = sb("gate_c", [P, HC])
        up_c = sb("up_c", [P, HC])
        hid_s = sb("hid_s", [P, 4])
        st = sb("st", [P, 3, 6])
        mv = sb("mv", [P, 3, TC, 2])
        var = sb("var", [P, 3, TC])
        rstd = sb("rstd", [P, 3, TC])
        ab = sb("ab", [P, TC, 2])
        ms_eps = sb("ms_eps", [P, TC])
        w1t = sb("w1t", [P, 2, KC, H], F16)
        w3t = sb("w3t", [P, 2, KC, H], F16)
        w2t = sb("w2t", [P, 2, HC, D], F16)

        with ExitStack() as first:
            wft = sb("wft", [P, 2, KC, D], F16, first)
            wit = sb("wit", [P, 2, KC, D], F16, first)
            wgt = sb("wgt", [P, 2, KC, D], F16, first)
            wot = sb("wot", [P, 2, KC, D], F16, first)
            x_in = sb("x_in", [P, 2, D], F32, first)
            x_res = sb("x_res", [P, TC, D], F32, first)
            zn = sb("zn", [P, TC, D], F32, first)
            xnt = sb("xnt", [P, 2, KC, T], F16, first)
            ot = sb("ot", [P, 2, KC, T], F16, first)
            w_in = sb("w_in", [P, 2, D], F32, first)
            w_tr = sb("w_tr", [P, 2, KC, P], F32, first)
            w2a = sb("w2a", [P, HC, UW], F32, first)
            w2b = sb("w2b", [P, HC, UW], F32, first)
            x1t_st = sb("x1t_st", [P, 2, 2, KC, P], F16, first)
            gate = sb("gate", [P, T], F32, first)
            sg = sb("sg", [P, 2, T], F32, first)
            sl = sb("sl", [P, T], F32, first)
            o_s = sb("o_s", [P, 2, T], F32, first)
            osum = sb("osum", [P, T], F32, first)
            osq = sb("osq", [P, T], F32, first)
            gs = sb("gs", [P, 2, T], F32, first)
        with ExitStack() as second:
            x2t = sb("x2t", [P, B, TC, 2, KC, P], F16, second)
            x1r = sb("x1r", [P, TC, D], F32, second)
            row_c = sb("row_c", [P, D], F32, second)
            yv = sb("yv", [P, TC, D], F32, second)
            sga = sb("sga", [P, 2, T], F32, second)
            sil = sb("sil", [P, 2, T], F32, second)
            hd = sb("hd", [P, 2, T], F32, second)
            hsp = sb("hsp", [P, 2, 2, T], F16, second)

        ot_f32 = ot[:].rearrange("p s k t -> p (s k t)").bitcast(F32).rearrange("p (c d) -> p c d", c=KC)
        staged = (zn, x_res, ot_f32, zn)

        ps = [ctx.enter_context(nc.psum_tensor(f"ps{i}", [P, 512], F32)) for i in range(8)]

        ld_eye, ld_had, ld_gw = sem("ld_eye"), sem("ld_had"), sem("ld_gw")
        ld_x = [sem(f"ld_x{i}") for i in range(2)]
        ld_res = [sem(f"ld_res{i}") for i in range(TC)]
        ld_w13, ld_w13t, ld_w2, ld_x1r = sem("ld_w13"), sem("ld_w13t"), sem("ld_w2"), sem("ld_x1r")
        ld_x2t = [sem(f"ld_x2t{i}") for i in range(B)]
        ld_aw = [sem(f"ld_aw{i}") for i in range(4)]
        st_x1 = [sem(f"st_x1{i}") for i in range(TC)]
        st_x1t = [sem(f"st_x1t{i}") for i in range(2)]
        st_out = sem("st_out")
        ones_set, half_set = sem("ones_set"), sem("half_set")
        aw_sq, aw_scale, aw_mm, aw_hi, aw_lo = (sem(s) for s in (
            "aw_sq", "aw_scale", "aw_mm", "aw_hi", "aw_lo"))
        aw_srdy, w2_srdy = sem("aw_srdy"), sem("w2_srdy")
        part_max, all_max = sem("part_max"), sem("all_max")
        aw_chain, coef_chain, unscale_rdy, coef_rdy, yinv_rdy = (sem(s) for s in (
            "aw_chain", "coef_chain", "unscale_rdy", "coef_rdy", "yinv_rdy"))
        x_chain, x_var, x_rstd, x_norm, xt_mm, xt_hi, xt_lo = (sem(s) for s in (
            "x_chain", "x_var", "x_rstd", "x_norm", "xt_mm", "xt_hi", "xt_lo"))
        f_mm, i_mm, g_mm = sem("f_mm"), sem("i_mm"), sem("g_mm")
        gate_rdy, sgi_rdy, sgg_rdy, sli_rdy, nv_rdy, o_rdy, gs_rdy, op_rdy = (sem(s) for s in (
            "gate_rdy", "sgi_rdy", "sgg_rdy", "sli_rdy", "nv_rdy", "o_rdy", "gs_rdy", "op_rdy"))
        osq_rdy, oadd, o_hi, o_lo, ms_mm, e_rdy = (sem(s) for s in (
            "osq_rdy", "oadd", "o_hi", "o_lo", "ms_mm", "e_rdy"))
        y_mm, y_chain, y_var, y_rstd, y_ab, y_norm, x1_rdy = (sem(s) for s in (
            "y_mm", "y_chain", "y_var", "y_rstd", "y_ab", "y_norm", "x1_rdy"))
        y_scale = sem("y_scale")
        z_chain, z_var, z_rstd, z_norm, z_mm, z_hi, z_lo = (sem(s) for s in (
            "z_chain", "z_var", "z_rstd", "z_norm", "z_mm", "z_hi", "z_lo"))
        w_sq, w_max, w_chain, w_srdy, wt_hi, wt_lo = (sem(s) for s in (
            "w_sq", "w_max", "w_chain", "w_srdy", "wt_hi", "wt_lo"))
        w2_sq, w2_sum, w2_chain, w2_scaled, w2_fly, h2_mm, h2_hi, h2_lo = (sem(s) for s in (
            "w2_sq", "w2_sum", "w2_chain", "w2_scaled", "w2_fly", "h2_mm", "h2_hi", "h2_lo"))
        h_chain, hid_part, hid_max, hid_scale = (sem(s) for s in (
            "h_chain", "hid_part", "hid_max", "hid_scale"))
        ga_mm, up_mm, sga_rdy, sil_rdy, hid_rdy, hid_hi, hid_lo, d_mm = (sem(s) for s in (
            "ga_mm", "up_mm", "sga_rdy", "sil_rdy", "hid_rdy", "hid_hi", "hid_lo", "d_mm"))
        y_free, v_chain, v_var, v_rstd, v_ab, v_norm, out_rdy = (sem(s) for s in (
            "y_free", "v_chain", "v_var", "v_rstd", "v_ab", "v_norm", "out_rdy"))
        out_last = sem("out_last")

        def gates(b, c, after_f=(), after_i=(), after_g=()):
            return [("F", b, c), *after_f, ("I", b, c), *after_i, ("G", b, c), *after_g, ("O", b, c)]

        def butterflies(b, first_, last_):
            return [("FW", b, k) for k in range(first_, last_)]

        def first_chunks(b, z=((),) * 5, g0=(), g1=()):
            return gates(
                b, 0,
                [*z[0], ("WN", b, 0)],
                [*z[1], ("W2N", b, 0)],
                [*g0, *z[2], ("WT", b, 0), ("WN", b, 1)]
            ) + gates(
                b, 1,
                [*z[3]],
                [*z[4], ("WT", b, 1), ("WN", b, 2), *butterflies(b, 0, 2)],
                [*g1, ("WT", b, 2), ("WN", b, 3), *butterflies(b, 2, 5)])

        def last_chunks(b, last):
            n = b + 1
            more = [] if last else [("XL", n, 0), ("XL", n, 1)]
            stats = [] if last else [("X1", n, 0), ("X1", n, 1), ("X2", n, 0), ("X2", n, 1)]
            return more + gates(
                b, 2, [*butterflies(b, 5, 8), ("WT", b, 3)], [("H2", b, 0), ("H2", b, 1), ("W2N", b, 1)], []
            ) + gates(b, 3, butterflies(b, 8, 10), [*stats, *butterflies(b, 10, 12)], [])

        def projection(b, last):
            n = b + 1
            x = [[]] * 4 if last else [
                [("XT", n, 0), ("XT", n, 1)], [("X1", n, 2), ("X2", n, 2)], [("XT", n, 2), ("X1", n, 3), ("X2", n, 3)],
                [("XT", n, 3)]]
            return (x[0] + [("YA", b, 0)] + x[1] + butterflies(b, 12, 14) + [("YA", b, 1)] + x[2]
                    + butterflies(b, 14, 16) + [("YA", b, 2)] + x[3] + [("YA", b, 3), ("MS", b, 0)]
                    + [("Y", b, 0), ("Y", b, 1), ("YN", b, 0), ("Y", b, 2), ("YN", b, 1), ("Y", b, 3),
                       ("YN", b, 2), ("Z1", b, 0), ("YN", b, 3), ("Z1", b, 1)])

        def second_norm(b, last):
            again = lambda *tiles: [] if last else [("RL", b + 1, t) for t in tiles]
            return ([("Z2", b, 0), ("Z1", b, 2), ("H2", b, 2)],
                    [("Z2", b, 1), ("ZT", b, 0), ("Z1", b, 3), ("H2", b, 3)],
                    [("ZT", b, 1), ("Z2", b, 2), *again(0)],
                    [("Z2", b, 3), ("ZT", b, 2), *again(1)], [("ZT", b, 3), *again(2, 3)])

        def start():
            return ([("X1", 0, 0), ("X1", 0, 1), ("AS", 0, 0), ("X2", 0, 0), ("X2", 0, 1), ("XT", 0, 0), ("XT", 0, 1),
                     ("AS", 0, 1), ("AT", 0, 0), ("X1", 0, 2), ("X1", 0, 3), ("AS", 0, 2), ("X2", 0, 2), ("X2", 0, 3),
                     ("AT", 0, 1), ("XT", 0, 2), ("XT", 0, 3), ("GC", 0, 0), ("AT", 0, 2), ("RL", 0, 0), ("RL", 0, 1),
                     ("RL", 0, 2), ("RL", 0, 3)]
                    + first_chunks(0, g0=[("AS", 0, 3)], g1=[("AO", 0, t) for t in range(KC)]))

        def middle(b, last=False):
            z = second_norm(b, last)
            rest = [s for part in z for s in part] if last else first_chunks(b + 1, z)
            return last_chunks(b, last) + projection(b, last) + rest

        def first_half(eng, part):
            def do(steps):
                for kind, b, t in steps:
                    if kind in part:
                        part[kind](b, t)
            do(start())
            with eng.Fori(0, B - 1) as b:
                do(middle(b))
            do(middle(B - 1, last=True))

        small = ("XT", "AO", "H2", "ZT")
        uses = [s for s in start() + middle(0) + middle(1) + middle(2) + middle(3, True) if s[0] in small]
        bank_of = {s: 6 + n % 2 for n, s in enumerate(uses)}
        before = {s: uses[n - 2] for n, s in enumerate(uses) if n >= 2}
        for trip in range(1, B - 1):
            for (k, b, t), (_, b0, _) in zip(middle(trip), middle(0)):
                assert k not in small or bank_of[k, b, t] == bank_of[k, b0, t]

        def traced(b, b0=1):
            return b if isinstance(b, int) else b0

        def bank(kind, b, t):
            return ps[bank_of[kind, traced(b), t]]

        def quarters(bank_):
            return bank_[:].rearrange("p (k n) -> p k n", n=P)

        def h2_src(b, t):
            return bank("H2", b, t)[:].rearrange("p (c d) -> p c d", d=UW)

        def w2_dst(b, t):
            half = HC // 2 * (t % 2)
            return w2t[:, :, half:half + HC // 2, bass.ds((UB * b + t // 2) * UW, UW)]

        def first(b):
            return isinstance(b, int) and b == 0

        gate_bank, MEAN_BANK = ((4, 5, 0), (1, 2, 3)), 5

        def slot_uses(b, t):
            return TC // 2 * b + t // 2

        def row(ap, n):
            return ap[n] if isinstance(n, int) else ap[bass.ds(n, 1)].squeeze(0)

        block = ctx.enter_context(nc.Block())

        @block.sync
        def _(sp):
            def load_attention_weights(w, src):
                sp.dma_start(staged[w][:, :, :], src.rearrange("(c p) d -> p c d", p=P)).then_inc(ld_aw[w], 16)

            for t in range(2):
                sp.dma_start(x_in[:, t], x_rows[t]).then_inc(ld_x[t], 16)
            load_attention_weights(0, w_f)
            sp.dma_start(ident[:], eye).then_inc(ld_eye, 16)
            load_attention_weights(1, w_i)
            load_attention_weights(2, w_g)
            sp.dma_start(gw[:], gnorm).then_inc(ld_gw, 16)
            sp.dma_start(had[:], hadamard).then_inc(ld_had, 16)

            def load_x(b, t):
                if not (first(b) and t < 2):
                    sp.wait_ge(xt_mm, TC * b + t - 1)
                sp.dma_start(x_in[:, t % 2], row(x_rows, TC * b + t)).then_inc(ld_x[t % 2], 16)

            def xt(b, t):
                if t < 2:
                    load_x(b, t + 2)

            def output_gate(b, t):
                sp.wait_ge(aw_mm, KC)
                load_attention_weights(3, w_o)

            def load_w13(b, t):
                m = HQ * b + t
                if not (first(b) and t == 0):
                    sp.wait_ge(w_sq, 2 * m)
                for w, rows in enumerate((w1_rows, w3_rows)):
                    sp.dma_start(w_in[:, w], row(rows, m)).then_inc(ld_w13, 16)
                if not (first(b) and t == 0):
                    sp.wait_ge(wt_lo, m)
                for w, tiles in enumerate((w_1t, w_3t)):
                    sp.dma_start(w_tr[:, w], row(tiles, m)).then_inc(ld_w13t, 16)

            def load_w2(b, t):
                if not (first(b) and t == 0):
                    sp.wait_ge(h2_mm, 2 * (UB * b + t))
                sp.dma_start(w2a[:], row(w_2t, UB * b + t)).then_inc(ld_w2, 16)

            def load_res(b, t):
                if first(b):
                    sp.wait_ge(aw_mm, 2 * KC)
                else:
                    if t >= 2:
                        sp.wait_ge(st_x1t[t - 2], 16 * slot_uses(b, 0))
                    sp.wait_ge(st_x1[t], 16 * b)
                    sp.wait_ge(z_norm, TC * (b - 1) + t + 1)
                sp.dma_start(x_res[:, t], row(x_rows, TC * b + t)).then_inc(ld_res[t], 16)

            def yn(b, t):
                sp.wait_ge(x1_rdy, TC * b + t + 1)
                sp.dma_start(row(x1_rows, TC * b + t), x_res[:, t]).then_inc(st_x1[t], 16)

            def zt(b, t):
                sp.wait_ge(z_hi, TC * b + t + 1)
                sp.wait_ge(z_lo, TC * b + t + 1)
                sp.dma_start(row(x1t_dram, TC * b + t), x1t_st[:, t % 2]).then_inc(st_x1t[t % 2], 16)

            first_half(sp, {"XL": load_x, "XT": xt, "GC": output_gate, "WN": load_w13, "W2N": load_w2,
                            "RL": load_res, "YN": yn, "ZT": zt})

            for b in range(B):
                if b == 0:
                    sp.wait_ge(g_mm, B * KC)
                if b == B - 1:
                    sp.wait_ge(y_mm, B * TC)
                for slot in range(2):
                    sp.wait_ge(st_x1t[slot], 16 * slot_uses(b + 1, 0))
                sp.dma_start(x2t[:, b].rearrange("p t s k n -> p t (s k n)"),
                             x1t_dram[TC * b:TC * (b + 1)].rearrange("t p s k n -> p t (s k n)")
                             ).then_inc(ld_x2t[b], 16)
            sp.wait_ge(z_mm, B * TC)
            sp.wait_ge(z_lo, B * TC)
            for t in range(TC):
                sp.wait_ge(st_x1[t], 16 * B)

            def load_x1(b):
                sp.dma_start(x1r[:], x1_rows[bass.ds(TC * b, TC)].rearrange("t p d -> p t d")).then_inc(ld_x1r, 16)

            def store_out(b):
                for t in range(TC):
                    sp.wait_ge(out_rdy, TC * b + t + 1)
                    sp.dma_start(row(out_rows, TC * b + t), yv[:, t]).then_inc(st_out, 16)

            load_x1(0)
            with sp.Fori(0, B - 1) as b:
                store_out(b)
                sp.wait_ge(st_out, 16 * TC * (b + 1))
                load_x1(b + 1)
            for t in range(TC):
                sp.wait_ge(out_last, t + 1)
                sp.dma_start(out_rows[TC * (B - 1) + t], yv[:, t]).then_inc(st_out, 16)
            sp.wait_ge(st_out, 16 * B * TC)

        @block.tensor
        def _(pe):
            def three_passes(dst, a_hi, a_lo, b_hi, b_lo, start, stop):
                pe.matmul(dst, a_hi, b_hi, start=start, stop=False)
                pe.matmul(dst, a_hi, b_lo, start=False, stop=False)
                return pe.matmul(dst, a_lo, b_hi, start=False, stop=stop)

            def wait_small_bank(kind, b, t):
                key = (kind, traced(b), t)
                if key not in before:
                    return
                k, pb, pt = before[key]
                m = b + (pb - traced(b))
                if k == "XT":
                    pe.wait_ge(xt_lo, TC * m + pt + 1)
                elif k == "AO":
                    pe.wait_ge(aw_lo, 3 * KC + pt + 1)
                elif k == "H2":
                    pe.wait_ge(h2_lo, 4 * m + pt + 1)
                elif k == "ZT":
                    pe.wait_ge(z_lo, TC * m + pt + 1)

            def transpose_tile(dst, tile):
                for k in range(KC):
                    last = pe.transpose(dst[:, k * P:(k + 1) * P], tile[:, k * P:(k + 1) * P], ident[:])
                return last

            def xt(b, t):
                if first(b) and t == 0:
                    pe.wait_ge(ld_eye, 16)
                wait_small_bank("XT", b, t)
                pe.wait_ge(x_norm, TC * b + t + 1)
                transpose_tile(bank("XT", b, t), x_in[:, t % 2]).then_inc(xt_mm, 1)

            def attention_weights(b, w):
                for c in range(KC):
                    u = KC * w + c
                    if u >= KC:
                        pe.wait_ge(aw_lo, u - KC + 1)
                    pe.wait_ge(aw_scale, u + 1)
                    transpose_tile(ps[u % KC], staged[w][:, c]).then_inc(aw_mm, 1)

            def output_weights(b, c):
                wait_small_bank("AO", b, c)
                pe.wait_ge(aw_scale, 3 * KC + c + 1)
                transpose_tile(bank("AO", b, c), staged[3][:, c]).then_inc(aw_mm, 1)

            def project(c, kind, w_t, done):
                for k in range(KC):
                    last = three_passes(ps[gate_bank[c % 2][kind]][:], w_t[:, 0, k, c * P:(c + 1) * P],
                                        w_t[:, 1, k, c * P:(c + 1) * P], xnt[:, 0, k, :], xnt[:, 1, k, :],
                                        k == 0, k == KC - 1)
                last.then_inc(done, 1)

            def f(b, c):
                if c == 0:
                    pe.wait_ge(xt_hi, TC * (b + 1))
                    pe.wait_ge(xt_lo, TC * (b + 1))
                if first(b):
                    pe.wait_ge(aw_lo, 3 * KC)
                if c >= 2:
                    pe.wait_ge(gate_rdy, KC * b + c - 1)
                elif not first(b):
                    pe.wait_ge((gate_rdy, y_norm)[c], TC * b - (1, 2)[c])
                project(c, 0, wft, f_mm)

            def i(b, c):
                if c >= 2:
                    pe.wait_ge(sli_rdy, KC * b + c - 1)
                elif c == 0 and not first(b):
                    pe.wait_ge(e_rdy, b)
                elif not first(b):
                    pe.wait_ge(y_norm, TC * b - 1)
                project(c, 1, wit, i_mm)

            def g(b, c):
                if c >= 2:
                    pe.wait_ge(gs_rdy, KC * b + c - 1)
                elif not first(b):
                    pe.wait_ge(y_norm, TC * b - (3, 0)[c])
                project(c, 2, wgt, g_mm)

            def ms(b, t):
                pe.wait_ge(oadd, (KC - 1) * (b + 1))
                pe.wait_ge(sli_rdy, KC * b + 3)
                pe.wait_ge(ones_set, 1)
                for tt in range(TC):
                    last = pe.matmul(ps[MEAN_BANK][:, tt:tt + 1], osum[:, tt * P:(tt + 1) * P], ones[:],
                                     start=True, stop=True)
                last.then_inc(ms_mm, 1)

            def y_pass(t, k):
                return three_passes(ps[t][:], ot[:, 0, k, t * P:(t + 1) * P], ot[:, 1, k, t * P:(t + 1) * P],
                                    wot[:, 0, k, :], wot[:, 1, k, :], k == 0, k == KC - 1)

            def ya(b, t):
                if t == 0:
                    pe.wait_ge(aw_lo, 4 * KC)
                    pe.wait_ge(o_hi, KC * b + KC - 1)
                    pe.wait_ge(o_lo, KC * b + KC - 1)
                pe.wait_ge((gs_rdy, gate_rdy, sli_rdy, gs_rdy)[t], KC * b + (3, 4, 4, 4)[t])
                for k in range(KC - 1):
                    y_pass(t, k)

            def y(b, t):
                if t == 0:
                    pe.wait_ge(o_hi, KC * (b + 1))
                    pe.wait_ge(o_lo, KC * (b + 1))
                y_pass(t, KC - 1).then_inc(y_mm, 1)

            def zt(b, t):
                wait_small_bank("ZT", b, t)
                pe.wait_ge(z_norm, TC * b + t + 1)
                transpose_tile(bank("ZT", b, t), zn[:, t]).then_inc(z_mm, 1)

            def h2(b, t):
                if t == 0:
                    pe.wait_ge(ld_had, 16)
                if t < 2:
                    pe.wait_ge(wt_lo, HQ * b + 3)
                else:
                    wait_small_bank("H2", b, t)
                pe.wait_ge(w2_fly, 8 * (UB * b + t // 2 + 1))
                half = HC // 2 * (t % 2)
                pe.matmul(bank("H2", b, t)[:], had[:], w2a[:, half:half + HC // 2, :].rearrange("p c d -> p (c d)"),
                          start=True, stop=True).then_inc(h2_mm, 1)

            first_half(pe, {"XT": xt, "AT": attention_weights, "AO": output_weights, "F": f, "I": i, "G": g,
                            "MS": ms, "YA": ya, "Y": y, "ZT": zt, "H2": h2})

            def gate_up(b, c, s):
                n = HC * b + c
                for w_t, dst, free, done in ((w1t, ps[4 + s], sil_rdy, ga_mm), (w3t, ps[6 + s], hid_rdy, up_mm)):
                    if not (isinstance(n, int) and n < 2):
                        pe.wait_ge(free, n - 1)
                    for k in range(KC):
                        xs = [x2t[:, bass.ds(b, 1), :, h, k, :].squeeze(1) for h in range(2)]
                        ws = [w_t[:, h, k, bass.ds(c * P, P)] for h in range(2)]
                        last = three_passes(dst[:], ws[0], ws[1], xs[0], xs[1], k == 0, k == KC - 1)
                    last.then_inc(done, 1)

            def down(b, c, s, start=False, stop=False, each=False):
                n = HC * b + c
                pe.wait_ge(hid_hi, n + 1)
                pe.wait_ge(hid_lo, n + 1)
                if start:
                    pe.wait_ge(y_free, TC * b + 1)
                w_hi, w_lo = (w2t[:, h, bass.ds(c, 1), :].squeeze(1) for h in range(2))
                for t in range(TC):
                    last = three_passes(ps[t][:], hsp[:, s, 0, t * P:(t + 1) * P], hsp[:, s, 1, t * P:(t + 1) * P],
                                        w_hi, w_lo, start, stop)
                    if each:
                        last.then_inc(d_mm, 1)
                if not each:
                    last.then_inc(d_mm, 1)

            def batch_row(b, last):
                with pe.Fori(0, HC // 2 - 1) as j:
                    c = 2 * j + 1
                    gate_up(b, c + 1, 0)
                    down(b, c, 1)
                    gate_up(b, c + 2, 1)
                    down(b, c + 1, 0)
                if not last:
                    gate_up(b + 1, 0, 0)
                down(b, HC - 1, 1, stop=True, each=last)
                if not last:
                    gate_up(b + 1, 1, 1)
                    down(b + 1, 0, 0, start=True)

            pe.wait_ge(z_hi, B * TC)
            pe.wait_ge(z_lo, B * TC)
            pe.wait_ge(wt_lo, HC)
            pe.wait_ge(h2_lo, 2 * UNITS)
            pe.wait_ge(e_rdy, B)
            pe.wait_ge(gate_rdy, B * KC)
            pe.wait_ge(ld_x2t[0], 16)
            gate_up(0, 0, 0)
            gate_up(0, 1, 1)
            down(0, 0, 0, start=True)
            for b in range(1, B):
                pe.wait_ge(ld_x2t[b], 16)
            with pe.Fori(0, B - 1) as b:
                batch_row(b, False)
            batch_row(B - 1, True)

        @block.scalar
        def _(act):
            def xt(b, t):
                act.wait_ge(xt_mm, TC * b + t + 1)
                act.activation(xnt[:, 0, :, t * P:(t + 1) * P], quarters(bank("XT", b, t)), ACT.Copy).then_inc(xt_hi, 1)

            def square_attention_weights(b, w):
                act.wait_ge(ld_aw[w], 16)
                for c in range(KC):
                    act.wait_ge(aw_sq, KC * w + c)
                    act.activation(osq[:], staged[w][:, c], ACT.Square,
                                   accum_out=norm2[:, w, c:c + 1]).then_inc(aw_sq, 1)

            def attention_weights(b, w):
                for c in range(KC):
                    u = KC * w + c
                    act.wait_ge(aw_mm, u + 1)
                    act.activation((wft, wit, wgt)[w][:, 0, :, c * P:(c + 1) * P], quarters(ps[u % KC]),
                                   ACT.Copy).then_inc(aw_hi, 1)

            def output_weights(b, c):
                act.wait_ge(aw_mm, 3 * KC + c + 1)
                act.activation(wot[:, 0, :, c * P:(c + 1) * P], quarters(bank("AO", b, c)), ACT.Copy
                               ).then_inc(aw_hi, 1)

            def f(b, c):
                n = KC * b + c
                if first(b) and c == 0:
                    act.wait_ge(unscale_rdy, 3)
                act.wait_ge(f_mm, n + 1)
                if not (first(b) and c == 0):
                    act.wait_ge(o_rdy, n)
                act.activation(gate[:], ps[gate_bank[c % 2][0]][:], ACT.Sigmoid, scale=unscale[:, 0, c:c + 1]
                               ).then_inc(gate_rdy, 1)

            def i(b, c):
                n = KC * b + c
                act.wait_ge(i_mm, n + 1)
                act.wait_ge(sli_rdy, n)
                act.activation(sg[:, 0], ps[gate_bank[c % 2][1]][:], ACT.Sigmoid, scale=unscale[:, 1, c:c + 1]
                               ).then_inc(sgi_rdy, 1)

            def g(b, c):
                n = KC * b + c
                act.wait_ge(g_mm, n + 1)
                act.wait_ge(gs_rdy, n)
                act.activation(sg[:, 1], ps[gate_bank[c % 2][2]][:], ACT.Sigmoid, scale=unscale[:, 2, c:c + 1]
                               ).then_inc(sgg_rdy, 1)

            def o(b, c):
                n = KC * b + c
                act.wait_ge(o_rdy, n + 1)
                if c == 0:
                    act.wait_ge(ms_mm, b)
                else:
                    act.wait_ge(oadd, (KC - 1) * b + c - 1)
                act.activation(osum[:] if c == 0 else osq[:], o_s[:, c % 2], ACT.Square).then_inc(osq_rdy, 1)
                act.wait_ge(op_rdy, n + 1)
                act.activation(ot[:, 0, c, :], gs[:, c % 2], ACT.Copy).then_inc(o_hi, 1)

            def yn(b, t):
                act.wait_ge(y_ab, TC * b + t + 1)
                act.activation(zn[:, t], ps[t][:], ACT.Identity, bias=ab[:, t, 1:2], scale=ab[:, t, 0:1]
                               ).then_inc(y_norm, 1)

            def zt(b, t):
                act.wait_ge(z_mm, TC * b + t + 1)
                if t < 2:
                    act.wait_ge(ld_res[t + 2], 16 * (b + 1))
                else:
                    act.wait_ge(st_x1t[t % 2], 16 * slot_uses(b, t))
                act.activation(x1t_st[:, t % 2, 0], quarters(bank("ZT", b, t)), ACT.Copy).then_inc(z_hi, 1)

            def wn(b, t):
                m = HQ * b + t
                act.wait_ge(ld_w13, 32 * (m + 1))
                if not (first(b) and t == 0):
                    act.wait_ge(w_max, m)
                for w in range(2):
                    act.activation(w_in[:, w], w_in[:, w], ACT.Square, accum_out=wn2[:, w:w + 1]).then_inc(w_sq, 1)

            def wt(b, t):
                m = HQ * b + t
                act.wait_ge(w_srdy, m + 1)
                act.wait_ge(ld_w13t, 32 * (m + 1))
                for w, w_t in enumerate((w1t, w3t)):
                    act.activation(w_t[:, 0, :, bass.ds(m * P, P)], w_tr[:, w], ACT.Copy, scale=w_s[:, w:w + 1]
                                   ).then_inc(wt_hi, 1)

            def w2n(b, t):
                m = UB * b + t
                act.wait_ge(ld_w2, 16 * (m + 1))
                if not (first(b) and t == 0):
                    act.wait_ge(w2_sum, m)
                act.activation(w2b[:], w2a[:], ACT.Square, accum_out=w2n2[:, 0:1]).then_inc(w2_sq, 1)

            def h2(b, t):
                act.wait_ge(h2_mm, 2 * UB * b + t + 1)
                act.activation(w2_dst(b, t)[:, 0], h2_src(b, t), ACT.Copy).then_inc(h2_hi, 1)

            first_half(act, {"XT": xt, "AS": square_attention_weights, "AT": attention_weights,
                             "AO": output_weights, "F": f, "I": i, "G": g, "O": o, "YN": yn, "ZT": zt,
                             "WN": wn, "WT": wt, "W2N": w2n, "H2": h2})

            def gate_up(b, c, s):
                n = HC * b + c
                act.wait_ge(ga_mm, n + 1)
                if not (isinstance(n, int) and n < 2):
                    act.wait_ge(sil_rdy, n - 1)
                act.activation(sga[:, s], ps[4 + s][:], ACT.Sigmoid, scale=gate_c[:, bass.ds(c, 1)]
                               ).then_inc(sga_rdy, 1)
                act.wait_ge(hid_rdy, n + 1)
                if not (isinstance(n, int) and n < 2):
                    act.wait_ge(d_mm, n - 1)
                act.activation(hsp[:, s, 0], hd[:, s], ACT.Copy).then_inc(hid_hi, 1)

            def norm_out(b, t):
                act.activation(yv[:, t], yv[:, t], ACT.Identity, bias=ab[:, t, 1:2], scale=rstd[:, 1, t:t + 1]
                               ).then_inc(v_norm, 1)

            def batch_row(b, last):
                with act.Fori(0, HC // 2 - 1) as j:
                    c = 2 * j + 1
                    gate_up(b, c + 1, 0)
                    gate_up(b, c + 2, 1)
                if not last:
                    gate_up(b + 1, 0, 0)
                    gate_up(b + 1, 1, 1)
                    act.wait_ge(v_ab, b + 1)
                for t in range(TC):
                    if last:
                        act.wait_ge(v_ab, b + t + 1)
                    norm_out(b, t)

            act.wait_ge(hid_scale, 2)
            act.wait_ge(z_lo, B * TC)
            act.wait_ge(o_lo, B * KC)
            act.wait_ge(x1_rdy, B * TC)
            for slot in range(2):
                act.wait_ge(st_x1t[slot], 16 * slot_uses(B, 0))
            for t in range(TC):
                act.wait_ge(st_x1[t], 16 * B)
            gate_up(0, 0, 0)
            gate_up(0, 1, 1)
            with act.Fori(0, B - 1) as b:
                batch_row(b, False)
            batch_row(B - 1, True)

        @block.vector
        def _(dve):
            dve.memset(ones[:], 1.0).then_inc(ones_set, 1)
            dve.memset(neg_half[:], -0.5).then_inc(half_set, 1)

            def exponent_scales(sem_, base, norm, exp, s, inv, done, done_at):
                dve.tensor_scalar(exp.bitcast(I32), norm.bitcast(I32), 24, None, ALU.logical_shift_right
                                  ).then_inc(sem_, 1)
                dve.wait_ge(sem_, base + 1)
                dve.tensor_scalar(exp.bitcast(I32), exp.bitcast(I32), float(F_LEAST), None, ALU.max
                                  ).then_inc(sem_, 1)
                dve.wait_ge(sem_, base + 2)
                dve.tensor_scalar(inv.bitcast(I32), exp.bitcast(I32), BIT, (127 - ROW_EXP) * BIT, ALU.mult, ALU.add
                                  ).then_inc(sem_, 1)
                dve.tensor_scalar(s.bitcast(I32), exp.bitcast(I32), -BIT, (127 + ROW_EXP) * BIT, ALU.mult, ALU.add
                                  ).then_inc(done, 1)
                dve.wait_ge(done, done_at)

            def row_stats(sem_, base, src, which, t):
                dve.bn_stats(st[:, which], src).then_inc(sem_, 1)
                dve.drain()
                dve.bn_aggr(mv[:, which, t], st[:, which]).then_inc(sem_, 1)
                dve.wait_ge(sem_, base + 2)

            def x1(b, t):
                m = TC * b + t
                dve.wait_ge(ld_x[t % 2], 16 * (slot_uses(b, t) + 1))
                row_stats(x_chain, 2 * m, x_in[:, t % 2], 0, t)
                dve.tensor_scalar(var[:, 0, t:t + 1], mv[:, 0, t, 1:2], EPS, 2.0 ** (-2 * X_EXP), ALU.add, ALU.mult
                                  ).then_inc(x_var, 1)

            def x2(b, t):
                m = TC * b + t
                dve.wait_ge(x_rstd, m + 1)
                dve.tensor_scalar(x_in[:, t % 2], x_in[:, t % 2], mv[:, 0, t, 0:1], rstd[:, 0, t:t + 1],
                                  ALU.subtract, ALU.mult).then_inc(x_norm, 1)

            def xt(b, t):
                dve.wait_ge(xt_hi, TC * b + t + 1)
                dve.tensor_tensor(xnt[:, 1, :, t * P:(t + 1) * P], quarters(bank("XT", b, t)),
                                  xnt[:, 0, :, t * P:(t + 1) * P], ALU.subtract).then_inc(xt_lo, 1)

            def split_attention_weights(b, w):
                for c in range(KC):
                    u, w_t = KC * w + c, (wft, wit, wgt)[w]
                    dve.wait_ge(aw_hi, u + 1)
                    dve.tensor_tensor(w_t[:, 1, :, c * P:(c + 1) * P], quarters(ps[u % KC]),
                                      w_t[:, 0, :, c * P:(c + 1) * P], ALU.subtract).then_inc(aw_lo, 1)

            def split_output_weights(b, c):
                dve.wait_ge(aw_hi, 3 * KC + c + 1)
                dve.tensor_tensor(wot[:, 1, :, c * P:(c + 1) * P], quarters(bank("AO", b, c)),
                                  wot[:, 0, :, c * P:(c + 1) * P], ALU.subtract).then_inc(aw_lo, 1)

            def scale_attention_weights(b, w):
                dve.wait_ge(aw_sq, KC * (w + 1))
                if w == 3:
                    return scale_output_weights()
                exponent_scales(aw_chain, 3 * w, norm2[:, w], s_tmp[:, 0:KC], row_s[:, w], row_inv[:, w],
                                aw_srdy, w + 1)
                for c in range(KC):
                    dve.tensor_scalar(staged[w][:, c], staged[w][:, c], row_s[:, w, c:c + 1], None, ALU.mult
                                      ).then_inc(aw_scale, 1)
                dve.tensor_scalar(unscale[:, w], row_inv[:, w], 2.0 ** -X_EXP, None, ALU.mult).then_inc(unscale_rdy, 1)

            def gate_coefficients(b, t):
                dve.wait_ge(ld_gw, 16)
                dve.tensor_tensor(g_coef[:], row_inv[:, 1], row_inv[:, 2], ALU.mult).then_inc(coef_chain, 1)
                dve.wait_ge(coef_chain, 1)
                dve.tensor_tensor(g_coef[:], g_coef[:], gw[:], ALU.mult).then_inc(coef_chain, 1)
                dve.wait_ge(coef_chain, 2)
                dve.tensor_scalar(g_coef[:].bitcast(I32), g_coef[:].bitcast(I32), 0x7FFFFFFF, None, ALU.bitwise_and
                                  ).then_inc(coef_chain, 1)
                dve.wait_ge(coef_chain, 3)
                dve.tensor_reduce(s_tmp[:, 5:6], g_coef[:], AX.X, ALU.max).then_inc(part_max, 1)
                o_exp = 126 - NORM_BOUND_EXP + HID_EXP
                dve.wait_ge(all_max, 1)
                dve.tensor_scalar(s_tmp[:, 1:2].bitcast(I32), s_tmp[:, 7:8].bitcast(I32), 23, None,
                                  ALU.logical_shift_right).then_inc(coef_chain, 1)
                dve.wait_ge(coef_chain, 4)
                dve.tensor_scalar(s_tmp[:, 2:3].bitcast(I32), s_tmp[:, 1:2].bitcast(I32), -BIT, (127 + o_exp) * BIT,
                                  ALU.mult, ALU.add).then_inc(coef_chain, 1)
                dve.tensor_scalar(s_tmp[:, 3:4].bitcast(I32), s_tmp[:, 1:2].bitcast(I32), BIT, (127 - o_exp) * BIT,
                                  ALU.mult, ALU.add).then_inc(coef_chain, 1)
                dve.wait_ge(coef_chain, 6)
                dve.scalar_tensor_tensor(g_coef[:], gw[:], s_tmp[:, 2:3], unscale[:, 2], ALU.mult, ALU.mult
                                         ).then_inc(coef_chain, 1)
                dve.wait_ge(coef_chain, 7)
                dve.tensor_scalar(g_coef[:], g_coef[:], -1.0, None, ALU.mult).then_inc(coef_rdy, 1)
                dve.wait_ge(coef_rdy, 1)

            def scale_output_weights():
                w = 3
                dve.tensor_reduce(s_tmp[:, 4:5], norm2[:, w], AX.X, ALU.max).then_inc(part_max, 1)
                dve.wait_ge(all_max, 2)
                exponent_scales(aw_chain, 9, s_tmp[:, 6:7], s_tmp[:, 0:1], row_s[:, w, 0:1], row_inv[:, w, 0:1],
                                aw_srdy, 4)
                for c in range(KC):
                    dve.tensor_scalar(staged[w][:, c], staged[w][:, c], row_s[:, w, 0:1], None, ALU.mult
                                      ).then_inc(aw_scale, 1)
                dve.tensor_tensor(y_inv[:, 0:1], s_tmp[:, 3:4], row_inv[:, w, 0:1], ALU.mult).then_inc(coef_chain, 1)
                dve.wait_ge(coef_chain, 8)
                dve.tensor_tensor(y_inv[:, 1:2], y_inv[:, 0:1], y_inv[:, 0:1], ALU.mult).then_inc(yinv_rdy, 1)
                dve.wait_ge(yinv_rdy, 1)

            def i(b, c):
                n = KC * b + c
                dve.wait_ge(sgi_rdy, n + 1)
                dve.scalar_tensor_tensor(sl[:], ps[gate_bank[c % 2][1]][:], unscale[:, 1, c:c + 1], sg[:, 0],
                                         ALU.mult, ALU.mult).then_inc(sli_rdy, 1)
                dve.wait_ge(sli_rdy, n + 1)
                dve.wait_ge(gate_rdy, n + 1)
                dve.scalar_tensor_tensor(sl[:], gate[:], 1.0, sl[:], ALU.subtract, ALU.mult
                                         ).then_inc(nv_rdy, 1)
                dve.wait_ge(nv_rdy, n + 1)
                if not (first(b) and c < 2):
                    dve.wait_ge(osq_rdy, n - 1)
                dve.tensor_tensor_scan(o_s[:, c % 2], gate[:], sl[:], 0.0, ALU.mult, ALU.add
                                       ).then_inc(o_rdy, 1)

            def g(b, c):
                n = KC * b + c
                dve.wait_ge(sgg_rdy, n + 1)
                if not (first(b) and c < 2):
                    dve.wait_ge(o_lo, n - 1)
                dve.scalar_tensor_tensor(gs[:, c % 2], ps[gate_bank[c % 2][2]][:], g_coef[:, c:c + 1], sg[:, 1],
                                         ALU.mult, ALU.mult).then_inc(gs_rdy, 1)
                dve.wait_ge(gs_rdy, n + 1)
                dve.wait_ge(o_rdy, n + 1)
                dve.tensor_tensor(gs[:, c % 2], gs[:, c % 2], o_s[:, c % 2], ALU.mult).then_inc(op_rdy, 1)

            def ms(b, t):
                dve.wait_ge(ms_mm, b + 1)
                dve.tensor_scalar(ms_eps[:], ps[MEAN_BANK][:, 0:TC], EPS / D, EPS * EPS, ALU.mult, ALU.add).then_inc(e_rdy, 1)
                dve.wait_ge(e_rdy, b + 1)

            def y(b, t):
                m = TC * b + t
                dve.wait_ge(y_mm, m + 1)
                row_stats(y_chain, 2 * m, ps[t][:], 1, t)
                dve.scalar_tensor_tensor(var[:, 1, t:t + 1], mv[:, 1, t, 1:2], y_inv[:, 1:2], ms_eps[:, t:t + 1],
                                         ALU.mult, ALU.add).then_inc(y_var, 1)

            def yn(b, t):
                m = TC * b + t
                dve.wait_ge(y_rstd, m + 1)
                dve.tensor_scalar(ab[:, t, 0:1], rstd[:, 1, t:t + 1], y_inv[:, 0:1], None, ALU.mult
                                  ).then_inc(y_scale, 1)
                dve.wait_ge(y_scale, m + 1)
                dve.scalar_tensor_tensor(ab[:, t, 1:2], mv[:, 1, t, 0:1], -1.0, ab[:, t, 0:1], ALU.mult, ALU.mult
                                         ).then_inc(y_ab, 1)

            def z1(b, t):
                m = TC * b + t
                dve.wait_ge(x1_rdy, m + 1)
                row_stats(z_chain, 2 * m, x_res[:, t], 2, t)
                dve.tensor_scalar(var[:, 2, t:t + 1], mv[:, 2, t, 1:2], EPS, 2.0 ** (-2 * X_EXP), ALU.add, ALU.mult
                                  ).then_inc(z_var, 1)

            def z2(b, t):
                m = TC * b + t
                dve.wait_ge(z_rstd, m + 1)
                dve.tensor_scalar(zn[:, t], x_res[:, t], mv[:, 2, t, 0:1], rstd[:, 2, t:t + 1],
                                  ALU.subtract, ALU.mult).then_inc(z_norm, 1)

            def zt(b, t):
                dve.wait_ge(z_hi, TC * b + t + 1)
                dve.tensor_tensor(x1t_st[:, t % 2, 1], quarters(bank("ZT", b, t)), x1t_st[:, t % 2, 0], ALU.subtract
                                  ).then_inc(z_lo, 1)

            def wn(b, t):
                m = HQ * b + t
                dve.wait_ge(w_max, m + 1)
                if not (first(b) and t == 0):
                    dve.wait_ge(wt_hi, 2 * m)
                    dve.wait_ge(wt_lo, m)
                exponent_scales(w_chain, 3 * m, wmax[:], wexp[:], w_s[:], w13_inv[:, :, bass.ds(m, 1)].squeeze(2),
                                w_srdy, m + 1)

            def wt(b, t):
                m = HQ * b + t
                for w, w_t in enumerate((w1t, w3t)):
                    dve.wait_ge(wt_hi, 2 * m + w + 1)
                    last = dve.scalar_tensor_tensor(w_t[:, 1, :, bass.ds(m * P, P)], w_tr[:, w], w_s[:, w:w + 1],
                                                    w_t[:, 0, :, bass.ds(m * P, P)], ALU.mult, ALU.subtract)
                last.then_inc(wt_lo, 1)

            def w2n(b, t):
                m = UB * b + t
                dve.wait_ge(w2_sum, m + 1)
                exponent_scales(w2_chain, 3 * m, w2n2[:, 1:2], w2exp[:], w2_s[:], w2_inv[:, bass.ds(m, 1)],
                                w2_srdy, m + 1)
                dve.tensor_scalar(w2a[:], w2a[:], w2_s[:], 2.0 ** -5, ALU.mult, ALU.mult).then_inc(w2_scaled, 1)

            def h2(b, t):
                dve.wait_ge(h2_hi, 2 * UB * b + t + 1)
                dst = w2_dst(b, t)
                dve.tensor_tensor(dst[:, 1], h2_src(b, t), dst[:, 0], ALU.subtract).then_inc(h2_lo, 1)

            first_half(dve, {"X1": x1, "X2": x2, "XT": xt, "AS": scale_attention_weights,
                             "AT": split_attention_weights, "GC": gate_coefficients, "AO": split_output_weights,
                             "I": i, "G": g, "MS": ms, "Y": y, "YN": yn, "Z1": z1, "Z2": z2, "ZT": zt,
                             "WN": wn, "WT": wt, "W2N": w2n, "H2": h2})

            dve.tensor_tensor(up_c[:], w13_inv[:, 0], w13_inv[:, 1], ALU.mult).then_inc(h_chain, 1)
            dve.wait_ge(h_chain, 1)
            dve.tensor_reduce(hid_s[:, 0:1], up_c[:], AX.X, ALU.max).then_inc(hid_part, 1)
            dve.wait_ge(hid_max, 1)
            dve.tensor_scalar(hid_s[:, 2:3].bitcast(I32), hid_s[:, 1:2].bitcast(I32), -1.0,
                              (2 * 127 - NORM_BOUND_EXP + HID_EXP) * BIT, ALU.mult, ALU.add).then_inc(h_chain, 1)
            dve.wait_ge(h_chain, 2)
            dve.tensor_scalar(up_c[:], w13_inv[:, 1], hid_s[:, 2:3], 2.0 ** -X_EXP, ALU.mult, ALU.mult
                              ).then_inc(hid_scale, 1)
            dve.tensor_scalar(gate_c[:], w13_inv[:, 0], 2.0 ** -X_EXP, None, ALU.mult).then_inc(hid_scale, 1)
            dve.wait_ge(o_lo, B * KC)
            dve.wait_ge(x1_rdy, B * TC)
            dve.wait_ge(z_mm, B * TC)
            for slot in range(2):
                dve.wait_ge(st_x1t[slot], 16 * slot_uses(B, 0))
            for t in range(TC):
                dve.wait_ge(st_x1[t], 16 * B)

            def gate_up(b, c, s):
                n = HC * b + c
                dve.wait_ge(sga_rdy, n + 1)
                dve.scalar_tensor_tensor(sil[:, s], ps[4 + s][:], gate_c[:, bass.ds(c, 1)], sga[:, s],
                                         ALU.mult, ALU.mult).then_inc(sil_rdy, 1)
                dve.wait_ge(sil_rdy, n + 1)
                dve.wait_ge(up_mm, n + 1)
                if not (isinstance(n, int) and n < 2):
                    dve.wait_ge(hid_lo, n - 1)
                dve.scalar_tensor_tensor(hd[:, s], ps[6 + s][:], up_c[:, bass.ds(c, 1)], sil[:, s],
                                         ALU.mult, ALU.mult).then_inc(hid_rdy, 1)

            def unscale_out(b, t):
                dve.tensor_tensor(yv[:, t], ps[t][:], row_c[:], ALU.mult).then_inc(y_free, 1)

            def out_shift(t0, t1):
                dve.scalar_tensor_tensor(ab[:, t0:t1, 1], mv[:, 1, t0:t1, 0], -1.0, rstd[:, 1, t0:t1],
                                         ALU.mult, ALU.mult).then_inc(v_ab, 1)

            def out_var(t0, t1):
                dve.tensor_scalar(var[:, 1, t0:t1], mv[:, 1, t0:t1, 1], EPS, None, ALU.add).then_inc(v_var, 1)

            def norm_out(b):
                for t in range(TC):
                    dve.wait_ge(y_free, TC * b + t + 2)
                    row_stats(v_chain, 2 * (TC * b + t), yv[:, t], 1, t)
                out_var(0, TC)
                dve.wait_ge(v_rstd, b + 1)
                out_shift(0, TC)

            def last_out(b, t):
                if t < TC:
                    dve.wait_ge(d_mm, HC * (b + 1) + t)
                    unscale_out(b, t)
                    dve.wait_ge(y_free, TC * b + t + 2)
                    row_stats(v_chain, 2 * (TC * b + t), yv[:, t], 1, t)
                    out_var(t, t + 1)
                if 1 <= t <= TC:
                    dve.wait_ge(v_rstd, b + t)
                    out_shift(t - 1, t)
                if t >= 2:
                    dve.wait_ge(v_norm, TC * b + t - 1)
                    dve.tensor_tensor(yv[:, t - 2], yv[:, t - 2], x1r[:, t - 2], ALU.add).then_inc(out_last, 1)

            def batch_row(b, last):
                with dve.Fori(0, HC // 2 - 1) as j:
                    c = 2 * j + 1
                    gate_up(b, c + 1, 0)
                    gate_up(b, c + 2, 1)
                if not last:
                    gate_up(b + 1, 0, 0)
                dve.wait_ge(ld_x1r, 16 * (b + 1))
                if last:
                    for t in range(TC + 2):
                        last_out(b, t)
                else:
                    dve.wait_ge(d_mm, HC * (b + 1))
                    for t in range(TC):
                        unscale_out(b, t)
                    gate_up(b + 1, 1, 1)
                    norm_out(b)

            dve.wait_ge(hid_scale, 2)
            out_scale = 2.0 ** (NORM_BOUND_EXP - HID_EXP + 5) * float(np.float32(1.0 / np.sqrt(H)))
            dve.tensor_scalar(w2_inv[:], w2_inv[:], hid_s[:, 1:2], out_scale, ALU.mult, ALU.mult
                              ).then_inc(h_chain, 1)
            dve.wait_ge(h_chain, 3)
            dve.tensor_copy(row_c[:].rearrange("p (u d) -> p u d", d=UW),
                            w2_inv[:].rearrange("p (u o) -> p u o", o=1).broadcast_to((P, UNITS, UW))
                            ).then_inc(y_free, 1)
            dve.wait_ge(y_free, 1)
            gate_up(0, 0, 0)
            gate_up(0, 1, 1)
            with dve.Fori(0, B - 1) as b:
                batch_row(b, False)
            batch_row(B - 1, True)

        @block.gpsimd
        def _(pool):
            def rsqrt(dst, src, done):
                pool.tensor_tensor(dst, src, neg_half[:].broadcast_to(src.shape), ALU.pow).then_inc(done, 1)

            def x1(b, t):
                pool.wait_ge(x_var, TC * b + t + 1)
                if first(b) and t == 0:
                    pool.wait_ge(half_set, 1)
                    pool.wait_ge(ones_set, 1)
                rsqrt(rstd[:, 0, t:t + 1], var[:, 0, t:t + 1], x_rstd)

            def output_weights(b, t):
                pool.wait_ge(part_max, 2)
                pool.partition_all_reduce(s_tmp[:, 6:7], s_tmp[:, 4:5], P, RMAX).then_inc(all_max, 1)

            def gate_coefficients(b, t):
                pool.wait_ge(part_max, 1)
                pool.partition_all_reduce(s_tmp[:, 7:8], s_tmp[:, 5:6], P, RMAX).then_inc(all_max, 1)

            def o(b, c):
                n = KC * b + c
                if c > 0:
                    pool.wait_ge(osq_rdy, n + 1)
                    pool.wait_ge(oadd, (KC - 1) * b + c - 1)
                    pool.tensor_tensor(osum[:], osum[:], osq[:], ALU.add).then_inc(oadd, 1)
                pool.wait_ge(o_hi, n + 1)
                pool.tensor_tensor(ot[:, 1, c, :], gs[:, c % 2], ot[:, 0, c, :], ALU.subtract).then_inc(o_lo, 1)

            def y(b, t):
                pool.wait_ge(y_var, TC * b + t + 1)
                rsqrt(rstd[:, 1, t:t + 1], var[:, 1, t:t + 1], y_rstd)

            def yn(b, t):
                pool.wait_ge(y_norm, TC * b + t + 1)
                pool.wait_ge(ld_res[t], 16 * (b + 1))
                pool.tensor_tensor(x_res[:, t], x_res[:, t], zn[:, t], ALU.add).then_inc(x1_rdy, 1)

            def z1(b, t):
                pool.wait_ge(z_var, TC * b + t + 1)
                rsqrt(rstd[:, 2, t:t + 1], var[:, 2, t:t + 1], z_rstd)

            def wn(b, t):
                m = HQ * b + t
                pool.wait_ge(w_sq, 2 * (m + 1))
                if not (first(b) and t == 0):
                    pool.wait_ge(w_srdy, m)
                pool.tensor_tensor(wn2_in[:], wn2[:], ones[:].broadcast_to((P, 2)), ALU.mult)
                pool.drain()
                pool.partition_all_reduce(wmax[:], wn2_in[:], P, RMAX).then_inc(w_max, 1)

            def w2n(b, t):
                m = UB * b + t
                pool.wait_ge(w2_sq, m + 1)
                if not (first(b) and t == 0):
                    pool.wait_ge(w2_srdy, m)
                pool.tensor_tensor(w2n2[:, 2:3], w2n2[:, 0:1], ones[:], ALU.mult)
                pool.drain()
                pool.partition_all_reduce(w2n2[:, 1:2], w2n2[:, 2:3], P, RSUM).then_inc(w2_sum, 1)

            def fly(b, k):
                m, stage, half = UB * b + k // 8, k % 8 // 2, k % 2
                if k % 8 == 0:
                    pool.wait_ge(w2_scaled, m + 1)
                elif half == 0:
                    pool.wait_ge(w2_fly, 8 * UB * b + k)
                src, dst = (w2a, w2b) if stage % 2 == 0 else (w2b, w2a)
                s, d = (v[:].rearrange("p (g two w) d -> p g two (w d)", two=2, w=1 << stage) for v in (src, dst))
                pool.tensor_tensor(d[:, :, half], s[:, :, 0], s[:, :, 1], ALU.subtract if half else ALU.add
                                   ).then_inc(w2_fly, 1)

            first_half(pool, {"X1": x1, "AS": lambda b, w: output_weights(b, w) if w == 3 else None,
                              "GC": gate_coefficients, "O": o, "Y": y, "YN": yn, "Z1": z1, "WN": wn,
                              "W2N": w2n, "FW": fly})

            pool.wait_ge(hid_part, 1)
            pool.partition_all_reduce(hid_s[:, 1:2], hid_s[:, 0:1], P, RMAX).then_inc(hid_max, 1)

            def split(b, c, s):
                n = HC * b + c
                pool.wait_ge(hid_hi, n + 1)
                pool.tensor_tensor(hsp[:, s, 1], hd[:, s], hsp[:, s, 0], ALU.subtract).then_inc(hid_lo, 1)

            def residual(b):
                pool.wait_ge(v_var, b + 1)
                rsqrt(rstd[:, 1], var[:, 1], v_rstd)
                pool.wait_ge(ld_x1r, 16 * (b + 1))
                for t in range(TC):
                    pool.wait_ge(v_norm, TC * b + t + 1)
                    pool.tensor_tensor(yv[:, t], yv[:, t], x1r[:, t], ALU.add).then_inc(out_rdy, 1)

            def batch_row(b, last):
                with pool.Fori(0, HC // 2 - 1) as j:
                    c = 2 * j + 1
                    split(b, c + 1, 0)
                    split(b, c + 2, 1)
                if last:
                    for t in range(TC):
                        pool.wait_ge(v_var, b + t + 1)
                        rsqrt(rstd[:, 1, t:t + 1], var[:, 1, t:t + 1], v_rstd)
                else:
                    split(b + 1, 0, 0)
                    split(b + 1, 1, 1)
                    residual(b)

            split(0, 0, 0)
            split(0, 1, 1)
            with pool.Fori(0, B - 1) as b:
                batch_row(b, False)
            batch_row(B - 1, True)


_INS = ["L0_attn_hidden_states", "L0_attn_Wi", "L0_attn_Wf", "L0_attn_Wg", "L0_attn_Wo", "L0_attn_gnorm_w",
        "L0_ffn_W1", "L0_ffn_W2", "L0_ffn_W3"]


def kernel(**inputs):
    import concourse.bacc as bacc
    from concourse.bass_utils import run_bass_kernel_spmd

    nc = bacc.Bacc("TRN2", target_bir_lowering=False, num_devices=1)
    sign = np.ones((1, 1), np.float32)
    while sign.shape[0] < P:
        sign = np.block([[sign, sign], [sign, -sign]])
    arrays = {name: np.ascontiguousarray(inputs[name]) for name in _INS}
    arrays["gnorm"] = np.ascontiguousarray(arrays.pop("L0_attn_gnorm_w").reshape(-1, P).T)
    arrays["eye"] = np.eye(P, dtype=np.float32)
    arrays["hadamard"] = np.ascontiguousarray(sign)
    hc, kc = arrays["L0_ffn_W1"].shape[0] // P, arrays["L0_ffn_W1"].shape[1] // P
    for name in ("W1", "W3"):
        arrays[name + "t"] = np.ascontiguousarray(
            arrays["L0_ffn_" + name].reshape(hc, P, kc, P).transpose(0, 3, 2, 1))
    arrays["W2t"] = np.ascontiguousarray(
        arrays.pop("L0_ffn_W2").reshape(-1, UNIT_WIDTH, hc, P).transpose(0, 3, 2, 1))
    aps = {name: nc.dram_tensor(name, a.shape, mybir.dt.from_np(a.dtype), kind="ExternalInput").ap()
           for name, a in arrays.items()}
    out = nc.dram_tensor("out", arrays[_INS[0]].shape, F32, kind="ExternalOutput").ap()
    mixer_ffn_kernel(nc, aps["L0_attn_hidden_states"], aps["L0_attn_Wi"], aps["L0_attn_Wf"], aps["L0_attn_Wg"],
                     aps["L0_attn_Wo"], aps["gnorm"], aps["L0_ffn_W1"], aps["L0_ffn_W3"],
                     aps["W1t"], aps["W3t"], aps["W2t"], aps["eye"], aps["hadamard"], out)
    results = run_bass_kernel_spmd(nc, [arrays], core_ids=[0])
    return results.results[0]["out"]
```

```python
from contextlib import ExitStack

import numpy as np
import concourse.bass as bass
from concourse import mybir

ALU = mybir.AluOpType
ACT = mybir.ActivationFunctionType
AX = mybir.AxisListType
F32 = mybir.dt.float32
F16 = mybir.dt.float16
I32 = mybir.dt.int32
RMAX = bass.bass_isa.ReduceOp.max
RSUM = bass.bass_isa.ReduceOp.add

P = 128
UNIT_WIDTH = 64
EPS = 1e-5
X_EXP = 11
ROW_EXP = 77
F_LEAST = 24
BIT = float(1 << 23)
NORM_BOUND_EXP = 9 + 29
HID_EXP = 15


def mixer_ffn_kernel(nc, x, w_i, w_f, w_g, w_o, gnorm, w_13t, w_2t, eye, hadamard, out):
    B, T, D = x.shape
    H = w_13t.shape[0] * w_13t.shape[4]
    KC = D // P
    TC = T // P
    HC = H // P
    HQ = HC // B
    assert T == D == 512 and KC == TC == B == 4 and HC == 16

    x_rows = x.rearrange("b (t p) d -> (b t) p d", p=P)
    out_rows = out.rearrange("b (t p) d -> (b t) p d", p=P)
    UNITS, UW = w_2t.shape[0], w_2t.shape[3]
    UB = UNITS // B
    x1_rows = nc.dram_tensor("x1_rows", (B * TC, P, D), F32, kind="Internal").ap()
    x1t_dram = nc.dram_tensor("x1t_split", (B * TC, P, 2, KC, P), F16, kind="Internal").ap()

    with ExitStack() as ctx:
        def sb(name, shape, dt=F32, c=ctx):
            return c.enter_context(nc.sbuf_tensor(name, shape, dt))

        def sem(name):
            return ctx.enter_context(nc.semaphore(name))

        ident = sb("ident", [P, P])
        had = sb("had", [P, P])
        ones = sb("ones", [P, P])
        neg_half = sb("neg_half", [P, 1])
        gw = sb("gw", [P, KC])
        norm2 = sb("norm2", [P, 4, KC])
        norm2_part = sb("norm2_part", [P, 2, KC])
        row_s = sb("row_s", [P, 4, KC])
        row_inv = sb("row_inv", [P, 4, KC])
        unscale = sb("unscale", [P, 3, KC])
        g_coef = sb("g_coef", [P, KC])
        a_exp = sb("a_exp", [P, KC])
        s_tmp = sb("s_tmp", [P, 8])
        y_inv = sb("y_inv", [P, 2])
        wn2 = sb("wn2", [P, 2])
        wn2_in = sb("wn2_in", [P, 2])
        wsum = sb("wsum", [P, 2])
        wexp = sb("wexp", [P, 2])
        w_s = sb("w_s", [P, 2])
        w13_inv = sb("w13_inv", [P, 2, HC])
        w2n2 = sb("w2n2", [P, 3])
        w2exp = sb("w2exp", [P, 1])
        w2_s = sb("w2_s", [P, UB])
        w2_inv = sb("w2_inv", [P, UNITS])
        gate_c = sb("gate_c", [P, HC])
        up_c = sb("up_c", [P, HC])
        hid_s = sb("hid_s", [P, 4])
        st = sb("st", [P, 3, 6])
        mv = sb("mv", [P, 3, TC, 2])
        var = sb("var", [P, 3, TC])
        rstd = sb("rstd", [P, 3, TC])
        ab = sb("ab", [P, TC, 2])
        ms_eps = sb("ms_eps", [P, TC])
        w1t = sb("w1t", [P, 2, KC, H], F16)
        w3t = sb("w3t", [P, 2, KC, H], F16)
        w2t = sb("w2t", [P, 2, HC, D], F16)

        with ExitStack() as first:
            wft = sb("wft", [P, 2, KC, D], F16, first)
            wit = sb("wit", [P, 2, KC, D], F16, first)
            wgt = sb("wgt", [P, 2, KC, D], F16, first)
            wot = sb("wot", [P, 2, KC, D], F16, first)
            xnt = sb("xnt", [P, 2, KC, T], F16, first)
            ot = sb("ot", [P, 2, KC, T], F16, first)
            x_in = sb("x_in", [P, 2, D], F32, first)
            x_res = sb("x_res", [P, TC, D], F32, first)
            zn = sb("zn", [P, TC, D], F32, first)
            w_tr = sb("w_tr", [P, 2, 2, KC, P], F32, first)
            w2a = sb("w2a", [P, HC, UW], F32, first)
            w2b = sb("w2b", [P, HC, UW], F32, first)
            x1t_st = sb("x1t_st", [P, 2, 2, KC, P], F16, first)
            gate = sb("gate", [P, T], F32, first)
            sg = sb("sg", [P, 2, T], F32, first)
            sl = sb("sl", [P, T], F32, first)
            o_s = sb("o_s", [P, 2, T], F32, first)
            osum = sb("osum", [P, T], F32, first)
            osq = sb("osq", [P, T], F32, first)
            gs = sb("gs", [P, 2, T], F32, first)
        with ExitStack() as second:
            x2t = sb("x2t", [P, B, TC, 2, KC, P], F16, second)
            sga = sb("sga", [P, 2, T], F32, second)
            sil = sb("sil", [P, 2, T], F32, second)
            hd = sb("hd", [P, 2, T], F32, second)
            hsp = sb("hsp", [P, 2, 2, T], F16, second)
            x1r = sb("x1r", [P, TC, D], F32, second)
            row_c = sb("row_c", [P, D], F32, second)
            yv = sb("yv", [P, TC, D], F32, second)

        ot_f32 = ot[:].rearrange("p s k t -> p (s k t)").bitcast(F32).rearrange("p (c d) -> p c d", c=KC)
        staged = (zn, x_res, ot_f32, zn)
        split_w = (wft, wit, wgt, wot)
        w2b_halves = w2b[:].rearrange("p (two c) d -> p two (c d)", two=2)
        i_squares, g_squares = (gs[:, 0], gs[:, 1], o_s[:, 0], o_s[:, 1]), (
            w2b_halves[:, 0], w2b_halves[:, 1], osum[:], osq[:])
        chain_start = (0, 3, 7, 11)

        w2_bufs = (w2a, w2b)

        ps = [ctx.enter_context(nc.psum_tensor(f"ps{i}", [P, 512], F32)) for i in range(8)]

        ld_eye, ld_had, ld_gw = sem("ld_eye"), sem("ld_had"), sem("ld_gw")
        ld_x = [sem(f"ld_x{i}") for i in range(2)]
        ld_res = [sem(f"ld_res{i}") for i in range(TC)]
        ld_w13 = [sem(f"ld_w13{i}") for i in range(2)]
        ld_w2 = [sem(f"ld_w2{i}") for i in range(2)]
        ld_x1r = sem("ld_x1r")
        ld_x2t = [sem(f"ld_x2t{i}") for i in range(B)]
        ld_aw = [sem(f"ld_aw{i}") for i in range(4)]
        st_x1 = [sem(f"st_x1{i}") for i in range(TC)]
        st_x1t = [sem(f"st_x1t{i}") for i in range(2)]
        st_out = sem("st_out")
        ones_set, half_set = sem("ones_set"), sem("half_set")
        aw_sq, aw_sq_act, aw_sum, aw_norm, aw_hi, aw_lo = (sem(s) for s in (
            "aw_sq", "aw_sq_act", "aw_sum", "aw_norm", "aw_hi", "aw_lo"))
        aw_srdy, w2_srdy = sem("aw_srdy"), sem("w2_srdy")
        part_max, all_max = sem("part_max"), sem("all_max")
        aw_chain, coef_chain, unscale_rdy, coef_rdy, yinv_rdy = (sem(s) for s in (
            "aw_chain", "coef_chain", "unscale_rdy", "coef_rdy", "yinv_rdy"))
        x_chain, x_var, x_rstd, x_norm, xt_mm, xt_hi, xt_lo = (sem(s) for s in (
            "x_chain", "x_var", "x_rstd", "x_norm", "xt_mm", "xt_hi", "xt_lo"))
        f_mm, i_mm, g_mm = sem("f_mm"), sem("i_mm"), sem("g_mm")
        gate_rdy, sgi_rdy, sgg_rdy, sli_rdy, nv_rdy, o_rdy, gs_rdy, op_rdy = (sem(s) for s in (
            "gate_rdy", "sgi_rdy", "sgg_rdy", "sli_rdy", "nv_rdy", "o_rdy", "gs_rdy", "op_rdy"))
        osq_rdy, oadd, o_hi, o_lo, ms_mm, e_rdy = (sem(s) for s in (
            "osq_rdy", "oadd", "o_hi", "o_lo", "ms_mm", "e_rdy"))
        y_mm, y_chain, y_var, y_rstd, y_ab, y_norm, x1_rdy = (sem(s) for s in (
            "y_mm", "y_chain", "y_var", "y_rstd", "y_ab", "y_norm", "x1_rdy"))
        y_scale = sem("y_scale")
        z_chain, z_var, z_rstd, z_norm, z_mm, z_hi, z_lo = (sem(s) for s in (
            "z_chain", "z_var", "z_rstd", "z_norm", "z_mm", "z_hi", "z_lo"))
        w_sq, w_sum, w_chain, w_srdy, wt_hi, wt_lo = (sem(s) for s in (
            "w_sq", "w_sum", "w_chain", "w_srdy", "wt_hi", "wt_lo"))
        w2_sq, w2_sum, w2_chain, w2_fly, h2_mm, h2_hi, h2_lo = (sem(s) for s in (
            "w2_sq", "w2_sum", "w2_chain", "w2_fly", "h2_mm", "h2_hi", "h2_lo"))
        h_chain, hid_part, hid_max, hid_scale = (sem(s) for s in (
            "h_chain", "hid_part", "hid_max", "hid_scale"))
        ga_mm, up_mm, sga_rdy, sil_rdy, hid_rdy, hid_hi, hid_lo, d_mm = (sem(s) for s in (
            "ga_mm", "up_mm", "sga_rdy", "sil_rdy", "hid_rdy", "hid_hi", "hid_lo", "d_mm"))
        y_free, v_chain, v_var, v_rstd, v_ab, v_norm, out_rdy = (sem(s) for s in (
            "y_free", "v_chain", "v_var", "v_rstd", "v_ab", "v_norm", "out_rdy"))
        out_last = sem("out_last")

        def gates(b, c, after_f=(), after_i=(), after_g=()):
            return [("F", b, c), *after_f, ("I", b, c), *after_i, ("G", b, c), *after_g, ("O", b, c)]

        def fly(b, *ks):
            return [("FW", b, k) for k in ks]

        def first_chunks(b, z):
            return (gates(b, 0, [*z[0], ("WN", b, 0)], [*z[1], ("WS", b, 0)], [*z[2], ("WT", b, 0)])
                    + gates(b, 1, [*z[3], ("WN", b, 1)], [*z[4], ("WS", b, 1)], [*z[5], ("WT", b, 1)])
                    + [*z[6], *fly(b, 0, 1), ("W2N", b, 0)])

        def last_chunks(b, last):
            n = b + 1
            loads = [] if last else [("XL", n, 0), ("XL", n, 1)]
            stats = [] if last else [("X1", n, 0), ("X1", n, 1)]
            norms = [] if last else [("X2", n, 0), ("X2", n, 1)]
            return (loads
                    + gates(b, 2, [("WN", b, 2), *fly(b, 2, 3)], [("WS", b, 2), *fly(b, 4)],
                            [*stats, ("WT", b, 2), *fly(b, 5)])
                    + gates(b, 3, [*norms, ("WN", b, 3), *fly(b, 6)], [("WS", b, 3), ("W2S", b, 0), *fly(b, 7)],
                            [("WT", b, 3)]))

        def projection(b, last):
            n = b + 1
            x = [[], [("HS", b, 0), ("X2L", b, 0)], [], [], []] if last else [
                [("XT", n, 0), ("XT", n, 1)], [("X1", n, 2), ("WL", n, 0)], [("X1", n, 3), ("X2", n, 2)],
                [("X2", n, 3), ("XT", n, 2)], [("XT", n, 3)]]
            return (x[0] + [("YA", b, 0), ("YA", b, 1)] + x[1] + fly(b, 8)
                    + [("YA", b, 2), ("H2", b, 0), ("H2", b, 1)] + x[2] + fly(b, 9)
                    + [("W2N", b, 1), ("YA", b, 3), ("MS", b, 0)] + x[3] + fly(b, 10)
                    + [("Y", b, 0), *x[4], ("Y", b, 1), ("YN", b, 0), ("Y", b, 2), ("YN", b, 1), ("Y", b, 3)]
                    + [("YN", b, 2), ("Z1", b, 0), ("YN", b, 3), ("Z1", b, 1)])

        def second_norm(b):
            again = [("RL", b + 1, t) for t in range(TC)]
            return ([("Z2", b, 0), ("Z1", b, 2), *fly(b, 11)],
                    [("Z2", b, 1), ("Z1", b, 3), *fly(b, 12, 13)],
                    [("ZT", b, 0), ("Z2", b, 2), *fly(b, 14)],
                    [("ZT", b, 1), ("Z2", b, 3), *fly(b, 15)],
                    [("ZT", b, 2), ("ZT", b, 3)],
                    [*again, ("W2S", b, 1)],
                    [("H2", b, 2), ("H2", b, 3)])

        def last_norm(b):
            return [("Z2", b, 0), ("GU", 0, 0), ("Z1", b, 2), ("Z2", b, 1), ("ZT", b, 0), ("Z1", b, 3), ("Z2", b, 2),
                    ("ZT", b, 1), ("Z2", b, 3), ("ZT", b, 2), *fly(b, 11, 12), ("ZT", b, 3), *fly(b, 13, 14, 15),
                    ("GU", 0, 1), ("W2S", b, 1), ("H2", b, 2), ("H2", b, 3)]

        def start():
            weights = ([("AN", 0, 2), ("AT", 0, 2), ("GC", 0, 0)], [("AQ", 0, 3)],
                       [("AR", 0, 3), *(("RL", 0, t) for t in range(TC))], [], [("AT", 0, 3)], [], [])
            return ([("X1", 0, 0), ("X1", 0, 1), ("X2", 0, 0), ("X2", 0, 1), ("XT", 0, 0), ("XT", 0, 1),
                     ("AQ", 0, 0), ("X1", 0, 2), ("AQ", 0, 1), ("X2", 0, 2), ("AR", 0, 0), ("X1", 0, 3),
                     ("AQ", 0, 2), ("X2", 0, 3), ("XT", 0, 2), ("XT", 0, 3), ("AT", 0, 0), ("AN", 0, 1), ("AT", 0, 1)]
                    + first_chunks(0, weights))

        def middle(b, last=False):
            rest = last_norm(b) if last else first_chunks(b + 1, second_norm(b))
            return last_chunks(b, last) + projection(b, last) + rest

        def first_half(eng, part):
            def do(steps):
                for kind, b, t in steps:
                    if kind in part:
                        part[kind](b, t)
            do(start())
            with eng.Fori(0, B - 1) as b:
                do(middle(b))
            do(middle(B - 1, last=True))

        small = ("XT", "AN", "H2", "ZT")
        uses = [s for s in start() + middle(0) + middle(1) + middle(2) + middle(3, True) if s[0] in small]
        bank_of = {s: 6 + n % 2 for n, s in enumerate(uses)}
        before = {s: uses[n - 2] for n, s in enumerate(uses) if n >= 2}
        for t in range(TC):
            bank_of["ZT", B - 1, t], before["ZT", B - 1, t] = t, ("YN", B - 1, t)
        for t in (2, 3):
            bank_of["H2", B - 1, t], before["H2", B - 1, t] = t - 2, ("ZT", B - 1, t - 2)
        for trip in range(1, B - 1):
            for (k, b, t), (_, b0, _) in zip(middle(trip), middle(0)):
                assert k not in small or bank_of[k, b, t] == bank_of[k, b0, t]

        def traced(b, b0=1):
            return b if isinstance(b, int) else b0

        def bank(kind, b, t):
            return ps[bank_of[kind, traced(b), t]]

        def quarters(bank_):
            return bank_[:].rearrange("p (k n) -> p k n", n=P)

        def h2_src(b, t):
            return bank("H2", b, t)[:].rearrange("p (c d) -> p c d", d=UW)

        def w2_dst(b, t):
            half = HC // 2 * (t % 2)
            return w2t[:, :, half:half + HC // 2, bass.ds((UB * b + t // 2) * UW, UW)]

        def first(b):
            return isinstance(b, int) and b == 0

        def is_last(b):
            return isinstance(b, int) and b == B - 1

        gate_bank, MEAN_BANK = ((4, 5, 0), (1, 2, 3)), 5

        def slot_uses(b, t):
            return TC // 2 * b + t // 2

        def row(ap, n):
            return ap[n] if isinstance(n, int) else ap[bass.ds(n, 1)].squeeze(0)

        block = ctx.enter_context(nc.Block())

        @block.sync
        def _(sp):
            def load_attention_weights(w, src):
                sp.dma_start(staged[w][:, :, :], src).then_inc(ld_aw[w], 16)

            sp.dma_start(x_in[:, 0], x_rows[0]).then_inc(ld_x[0], 16)
            sp.dma_start(ident[:], eye).then_inc(ld_eye, 16)
            sp.dma_start(x_in[:, 1], x_rows[1]).then_inc(ld_x[1], 16)
            load_attention_weights(0, w_f)
            load_attention_weights(1, w_i)

            def load_x(b, t):
                if not (first(b) and t < 2):
                    sp.wait_ge(xt_mm, TC * b + t - 1)
                sp.dma_start(x_in[:, t % 2], row(x_rows, TC * b + t)).then_inc(ld_x[t % 2], 16)

            def xt(b, t):
                if t < 2:
                    load_x(b, t + 2)
                if first(b) and t == 1:
                    load_attention_weights(2, w_g)
                    sp.dma_start(gw[:], gnorm).then_inc(ld_gw, 16)
                    load_w13(0, 0)
                    load_w13(0, 1)
                    sp.dma_start(w2a[:], w_2t[0]).then_inc(ld_w2[0], 16)
                    sp.dma_start(had[:], hadamard).then_inc(ld_had, 16)

            def output_weights(b, w):
                if w == 3:
                    sp.wait_ge(aw_lo, KC)
                    load_attention_weights(3, w_o)

            def load_w13(b, t):
                sp.dma_start(w_tr[:, t % 2], row(w_13t, HQ * b + t)).then_inc(ld_w13[t % 2], 16)

            def next_w13(b, t):
                if t < 2:
                    sp.wait_ge(wt_lo, HQ * b + t + 1)
                    load_w13(b, t + 2)

            def next_rows_w13(b, t):
                sp.wait_ge(wt_lo, HQ * b)
                load_w13(b, 0)
                load_w13(b, 1)

            def load_w2(b, k):
                if k == 7 or (k == 15 and not is_last(b)):
                    m = UB * b + k // 8 + 1
                    sp.wait_ge(w2_fly, 8 * m)
                    slot = (k // 8 + 1) % 2
                    sp.dma_start(w2_bufs[slot][:], row(w_2t, m)).then_inc(ld_w2[slot], 16)

            def load_res(b, t):
                if first(b):
                    sp.wait_ge(aw_lo, 2 * KC)
                else:
                    if t >= 2:
                        sp.wait_ge(st_x1t[t - 2], 16 * slot_uses(b, 0))
                    sp.wait_ge(st_x1[t], 16 * b)
                    sp.wait_ge(z_norm, TC * (b - 1) + t + 1)
                sp.dma_start(x_res[:, t], row(x_rows, TC * b + t)).then_inc(ld_res[t], 16)

            def yn(b, t):
                sp.wait_ge(x1_rdy, TC * b + t + 1)
                sp.dma_start(row(x1_rows, TC * b + t), x_res[:, t]).then_inc(st_x1[t], 16)

            def zt(b, t):
                sp.wait_ge(z_hi, TC * b + t + 1)
                sp.wait_ge(z_lo, TC * b + t + 1)
                sp.dma_start(row(x1t_dram, TC * b + t), x1t_st[:, t % 2]).then_inc(st_x1t[t % 2], 16)

            def load_x2t(b):
                if b == 0:
                    sp.wait_ge(g_mm, B * KC)
                if b == B - 1:
                    sp.wait_ge(y_mm, B * TC)
                for slot in range(2):
                    sp.wait_ge(st_x1t[slot], 16 * slot_uses(b + 1, 0))
                sp.dma_start(x2t[:, b].rearrange("p t s k n -> p t (s k n)"),
                             x1t_dram[TC * b:TC * (b + 1)].rearrange("t p s k n -> p t (s k n)")
                             ).then_inc(ld_x2t[b], 16)

            def start_second(b, t):
                for row_ in range(B - 1):
                    load_x2t(row_)

            first_half(sp, {"XL": load_x, "XT": xt, "AQ": output_weights, "WT": next_w13, "WL": next_rows_w13,
                            "FW": load_w2, "X2L": start_second,
                            "RL": load_res, "YN": yn, "ZT": zt})

            load_x2t(B - 1)
            sp.wait_ge(z_mm, B * TC)
            sp.wait_ge(z_lo, B * TC)
            for t in range(TC):
                sp.wait_ge(st_x1[t], 16 * B)

            def load_x1(b):
                sp.dma_start(x1r[:], x1_rows[bass.ds(TC * b, TC)].rearrange("t p d -> p t d")).then_inc(ld_x1r, 16)

            def store_out(b):
                for t in range(TC):
                    sp.wait_ge(out_rdy, TC * b + t + 1)
                    sp.dma_start(row(out_rows, TC * b + t), yv[:, t]).then_inc(st_out, 16)

            load_x1(0)
            with sp.Fori(0, B - 1) as b:
                store_out(b)
                sp.wait_ge(st_out, 16 * TC * (b + 1))
                load_x1(b + 1)
            for t in range(TC):
                sp.wait_ge(out_last, t + 1)
                sp.dma_start(out_rows[TC * (B - 1) + t], yv[:, t]).then_inc(st_out, 16)
            sp.wait_ge(st_out, 16 * B * TC)

        @block.tensor
        def _(pe):
            def three_passes(dst, a_hi, a_lo, b_hi, b_lo, start, stop):
                pe.matmul(dst, a_hi, b_hi, start=start, stop=False)
                pe.matmul(dst, a_hi, b_lo, start=False, stop=False)
                return pe.matmul(dst, a_lo, b_hi, start=False, stop=stop)

            def wait_small_bank(kind, b, t):
                key = (kind, traced(b), t)
                if key not in before:
                    return
                k, pb, pt = before[key]
                m = b + (pb - traced(b))
                if k == "XT":
                    pe.wait_ge(xt_lo, TC * m + pt + 1)
                elif k == "AN":
                    pe.wait_ge(aw_chain, chain_start[pt] + 1)
                elif k == "H2":
                    pe.wait_ge(h2_lo, 4 * m + pt + 1)
                elif k == "ZT":
                    pe.wait_ge(z_lo, TC * m + pt + 1)
                elif k == "YN":
                    pe.wait_ge(y_norm, TC * m + pt + 1)

            def transpose_tile(dst, tile):
                for k in range(KC):
                    last = pe.transpose(dst[:, k * P:(k + 1) * P], tile[:, k * P:(k + 1) * P], ident[:])
                return last

            def xt(b, t):
                if first(b) and t == 0:
                    pe.wait_ge(ld_eye, 16)
                if t < 2 and not first(b):
                    pe.wait_ge(wt_lo, HQ * (b - 1) + 3)
                else:
                    wait_small_bank("XT", b, t)
                pe.wait_ge(x_norm, TC * b + t + 1)
                transpose_tile(bank("XT", b, t), x_in[:, t % 2]).then_inc(xt_mm, 1)

            def norms(b, w):
                wait_small_bank("AN", b, w)
                if w == 1:
                    pe.wait_ge(ones_set, 1)
                for k in range(KC):
                    pe.wait_ge(*((aw_sq_act, KC + k + 1) if w == 1 else (aw_sq, k + 1)))
                    pe.matmul(bank("AN", b, w)[:], ones[:], (i_squares if w == 1 else g_squares)[k],
                              start=k == 0, stop=k == KC - 1).then_inc(aw_norm, 1)

            def project(c, kind, w_t, done):
                for k in range(KC):
                    last = three_passes(ps[gate_bank[c % 2][kind]][:], w_t[:, 0, k, c * P:(c + 1) * P],
                                        w_t[:, 1, k, c * P:(c + 1) * P], xnt[:, 0, k, :], xnt[:, 1, k, :],
                                        k == 0, k == KC - 1)
                last.then_inc(done, 1)

            def f(b, c):
                if c == 0:
                    pe.wait_ge(xt_hi, TC * (b + 1))
                    pe.wait_ge(xt_lo, TC * (b + 1))
                if first(b) and c == 0:
                    pe.wait_ge(aw_lo, KC)
                if c >= 2:
                    pe.wait_ge(gate_rdy, KC * b + c - 1)
                elif not first(b):
                    pe.wait_ge((gate_rdy, y_norm)[c], TC * b - (1, 2)[c])
                project(c, 0, wft, f_mm)

            def i(b, c):
                if c >= 2:
                    pe.wait_ge(sli_rdy, KC * b + c - 1)
                elif c == 0 and not first(b):
                    pe.wait_ge(e_rdy, b)
                elif not first(b):
                    pe.wait_ge(y_norm, TC * b - 1)
                if first(b) and c == 0:
                    pe.wait_ge(aw_lo, 2 * KC)
                project(c, 1, wit, i_mm)

            def g(b, c):
                if c >= 2:
                    pe.wait_ge(gs_rdy, KC * b + c - 1)
                elif not first(b):
                    pe.wait_ge(y_norm, TC * b - (3, 0)[c])
                if first(b) and c == 0:
                    pe.wait_ge(aw_lo, 3 * KC)
                project(c, 2, wgt, g_mm)

            def ms(b, t):
                pe.wait_ge(oadd, (KC - 1) * (b + 1))
                pe.wait_ge(sli_rdy, KC * b + 3)
                for tt in range(TC):
                    last = pe.matmul(ps[MEAN_BANK][:, tt:tt + 1], osum[:, tt * P:(tt + 1) * P], ones[:, 0:1],
                                     start=True, stop=True)
                last.then_inc(ms_mm, 1)

            def y_pass(t, k):
                return three_passes(ps[t][:], ot[:, 0, k, t * P:(t + 1) * P], ot[:, 1, k, t * P:(t + 1) * P],
                                    wot[:, 0, k, :], wot[:, 1, k, :], k == 0, k == KC - 1)

            def ya(b, t):
                if t == 0:
                    pe.wait_ge(aw_lo, 4 * KC)
                    pe.wait_ge(o_hi, KC * b + KC - 1)
                    pe.wait_ge(o_lo, KC * b + KC - 1)
                pe.wait_ge((gs_rdy, gate_rdy, sli_rdy, gs_rdy)[t], KC * b + (3, 4, 4, 4)[t])
                for k in range(KC - 1):
                    y_pass(t, k)

            def y(b, t):
                if t == 0:
                    pe.wait_ge(o_hi, KC * (b + 1))
                    pe.wait_ge(o_lo, KC * (b + 1))
                y_pass(t, KC - 1).then_inc(y_mm, 1)

            def zt(b, t):
                wait_small_bank("ZT", b, t)
                pe.wait_ge(z_norm, TC * b + t + 1)
                transpose_tile(bank("ZT", b, t), zn[:, t]).then_inc(z_mm, 1)

            def h2(b, t):
                if t == 0:
                    pe.wait_ge(ld_had, 16)
                wait_small_bank("H2", b, t)
                pe.wait_ge(w2_fly, 8 * (UB * b + t // 2 + 1))
                half = HC // 2 * (t % 2)
                pe.matmul(bank("H2", b, t)[:], had[:],
                          w2_bufs[t // 2][:, half:half + HC // 2, :].rearrange("p c d -> p (c d)"),
                          start=True, stop=True).then_inc(h2_mm, 1)

            def gate_up(b, c, s):
                n = HC * b + c
                for w_t, dst, free, done in ((w1t, ps[4 + s], sil_rdy, ga_mm), (w3t, ps[6 + s], hid_rdy, up_mm)):
                    if not (isinstance(n, int) and n < 2):
                        pe.wait_ge(free, n - 1)
                    for k in range(KC):
                        xs = [x2t[:, bass.ds(b, 1), :, h, k, :].squeeze(1) for h in range(2)]
                        ws = [w_t[:, h, k, bass.ds(c * P, P)] for h in range(2)]
                        last = three_passes(dst[:], ws[0], ws[1], xs[0], xs[1], k == 0, k == KC - 1)
                    last.then_inc(done, 1)

            def start_second(b, c):
                if c == 0:
                    pe.wait_ge(wt_lo, HC)
                    pe.wait_ge(ld_x2t[0], 16)
                pe.wait_ge((gate_rdy, e_rdy)[c], (B * KC - 1, B)[c])
                pe.wait_ge(h2_lo, 4 * (B - 1) + c + 1)
                gate_up(b, c, c)

            first_half(pe, {"XT": xt, "AN": norms, "F": f, "I": i, "G": g,
                            "GU": start_second, "MS": ms, "YA": ya, "Y": y, "ZT": zt, "H2": h2})

            def down(b, c, s, start=False, stop=False, each=False):
                n = HC * b + c
                pe.wait_ge(hid_hi, n + 1)
                pe.wait_ge(hid_lo, n + 1)
                if start:
                    pe.wait_ge(y_free, TC * b + 1)
                w_hi, w_lo = (w2t[:, h, bass.ds(c, 1), :].squeeze(1) for h in range(2))
                for t in range(TC):
                    last = three_passes(ps[t][:], hsp[:, s, 0, t * P:(t + 1) * P], hsp[:, s, 1, t * P:(t + 1) * P],
                                        w_hi, w_lo, start, stop)
                    if each:
                        last.then_inc(d_mm, 1)
                if not each:
                    last.then_inc(d_mm, 1)

            def batch_row(b, last):
                with pe.Fori(0, HC // 2 - 1) as j:
                    c = 2 * j + 1
                    gate_up(b, c + 1, 0)
                    down(b, c, 1)
                    gate_up(b, c + 2, 1)
                    down(b, c + 1, 0)
                if not last:
                    gate_up(b + 1, 0, 0)
                down(b, HC - 1, 1, stop=True, each=last)
                if not last:
                    gate_up(b + 1, 1, 1)
                    down(b + 1, 0, 0, start=True)

            pe.wait_ge(y_norm, B * TC)
            pe.wait_ge(z_lo, B * TC)
            pe.wait_ge(h2_lo, 2 * UNITS)
            down(0, 0, 0, start=True)
            for b in range(1, B):
                pe.wait_ge(ld_x2t[b], 16)
            with pe.Fori(0, B - 1) as b:
                batch_row(b, False)
            batch_row(B - 1, True)

        @block.scalar
        def _(act):
            def xt(b, t):
                act.wait_ge(xt_mm, TC * b + t + 1)
                act.activation(xnt[:, 0, :, t * P:(t + 1) * P], quarters(bank("XT", b, t)), ACT.Copy).then_inc(xt_hi, 1)

            def square_attention_weights(b, w):
                if w == 2:
                    return
                act.wait_ge(ld_aw[w], 16)
                if w == 3:
                    act.wait_ge(aw_norm, 2 * KC)
                for k in range(KC):
                    if w == 1:
                        act.activation(i_squares[k], staged[w][:, k], ACT.Square).then_inc(aw_sq_act, 1)
                        continue
                    if w == 3 and k >= 2:
                        act.wait_ge(aw_sq_act, 2 * KC + k - 1)
                    act.activation(g_squares[k % 2 if w == 3 else k].rearrange("p (k n) -> p k n", n=P),
                                   staged[w][:, :, k * P:(k + 1) * P], ACT.Square,
                                   accum_out=norm2_part[:, w // 3, k:k + 1]).then_inc(aw_sq_act, 1)

            def attention_weights(b, w):
                act.wait_ge(aw_srdy, w + 1)
                for c in range(KC):
                    scale_c = c if w < 3 else 0
                    act.activation(split_w[w][:, 0, :, c * P:(c + 1) * P], staged[w][:, :, c * P:(c + 1) * P], ACT.Copy,
                                   scale=row_s[:, w, scale_c:scale_c + 1]).then_inc(aw_hi, 1)

            def f(b, c):
                n = KC * b + c
                if first(b) and c == 0:
                    act.wait_ge(unscale_rdy, 1)
                act.wait_ge(f_mm, n + 1)
                if not (first(b) and c == 0):
                    act.wait_ge(o_rdy, n)
                act.activation(gate[:], ps[gate_bank[c % 2][0]][:], ACT.Sigmoid, scale=unscale[:, 0, c:c + 1]
                               ).then_inc(gate_rdy, 1)

            def i(b, c):
                n = KC * b + c
                if first(b) and c == 0:
                    act.wait_ge(unscale_rdy, 2)
                act.wait_ge(i_mm, n + 1)
                act.wait_ge(sli_rdy, n)
                act.activation(sg[:, 0], ps[gate_bank[c % 2][1]][:], ACT.Sigmoid, scale=unscale[:, 1, c:c + 1]
                               ).then_inc(sgi_rdy, 1)

            def g(b, c):
                n = KC * b + c
                if first(b) and c == 0:
                    act.wait_ge(unscale_rdy, 3)
                act.wait_ge(g_mm, n + 1)
                act.wait_ge(gs_rdy, n)
                act.activation(sg[:, 1], ps[gate_bank[c % 2][2]][:], ACT.Sigmoid, scale=unscale[:, 2, c:c + 1]
                               ).then_inc(sgg_rdy, 1)

            def o(b, c):
                n = KC * b + c
                act.wait_ge(o_rdy, n + 1)
                if c == 0:
                    act.wait_ge(ms_mm, b)
                else:
                    act.wait_ge(oadd, (KC - 1) * b + c - 1)
                act.activation(osum[:] if c == 0 else osq[:], o_s[:, c % 2], ACT.Square).then_inc(osq_rdy, 1)
                act.wait_ge(op_rdy, n + 1)
                act.activation(ot[:, 0, c, :], gs[:, c % 2], ACT.Copy).then_inc(o_hi, 1)

            def yn(b, t):
                act.wait_ge(y_ab, TC * b + t + 1)
                act.activation(zn[:, t], ps[t][:], ACT.Identity, bias=ab[:, t, 1:2], scale=ab[:, t, 0:1]
                               ).then_inc(y_norm, 1)

            def zt(b, t):
                act.wait_ge(z_mm, TC * b + t + 1)
                if t < 2:
                    act.wait_ge(ld_res[t + 2], 16 * (b + 1))
                else:
                    act.wait_ge(st_x1t[t % 2], 16 * slot_uses(b, t))
                act.activation(x1t_st[:, t % 2, 0], quarters(bank("ZT", b, t)), ACT.Copy).then_inc(z_hi, 1)

            def wn(b, t):
                m = HQ * b + t
                act.wait_ge(ld_w13[t % 2], 16 * (HQ // 2 * b + t // 2 + 1))
                if not (first(b) and t == 0):
                    act.wait_ge(w_sum, m)
                for w, w_t in enumerate((w1t, w3t)):
                    squares = w_t[:].rearrange("p s k n -> p (s k) n").bitcast(F32)[:, :, bass.ds(m * (P // 2), P // 2)]
                    chunk = w_tr[:, t % 2, w].rearrange("p k (two n) -> p (k two) n", two=2)
                    act.activation(squares, chunk, ACT.Square, accum_out=wn2[:, w:w + 1]).then_inc(w_sq, 1)

            def wt(b, t):
                m = HQ * b + t
                act.wait_ge(w_srdy, m + 1)
                for w, w_t in enumerate((w1t, w3t)):
                    act.activation(w_t[:, 0, :, bass.ds(m * P, P)], w_tr[:, t % 2, w], ACT.Copy, scale=w_s[:, w:w + 1]
                                   ).then_inc(wt_hi, 1)

            def w2n(b, t):
                m = UB * b + t
                act.wait_ge(ld_w2[t], 16 * (b + 1))
                if not (first(b) and t == 0):
                    act.wait_ge(w2_sum, m)
                squares = w2t[:].rearrange("p s c d -> p (s c) d").bitcast(F32)[:, :, bass.ds(m * (UW // 2), UW // 2)]
                unit = w2_bufs[t][:].rearrange("p c (two d) -> p (c two) d", two=2)
                act.activation(squares, unit, ACT.Square, accum_out=w2n2[:, 0:1]).then_inc(w2_sq, 1)

            def h2(b, t):
                act.wait_ge(h2_mm, 2 * UB * b + t + 1)
                act.wait_ge(w2_srdy, UB * b + t // 2 + 1)
                act.activation(w2_dst(b, t)[:, 0], h2_src(b, t), ACT.Copy, scale=w2_s[:, t // 2:t // 2 + 1]
                               ).then_inc(h2_hi, 1)

            def gate_up(b, c, s):
                n = HC * b + c
                act.wait_ge(ga_mm, n + 1)
                if not (isinstance(n, int) and n < 2):
                    act.wait_ge(sil_rdy, n - 1)
                act.activation(sga[:, s], ps[4 + s][:], ACT.Sigmoid, scale=gate_c[:, bass.ds(c, 1)]
                               ).then_inc(sga_rdy, 1)
                act.wait_ge(hid_rdy, n + 1)
                if not (isinstance(n, int) and n < 2):
                    act.wait_ge(d_mm, n - 1)
                act.activation(hsp[:, s, 0], hd[:, s], ACT.Copy).then_inc(hid_hi, 1)

            def start_second(b, c):
                if c == 0:
                    act.wait_ge(hid_scale, 2)
                    act.wait_ge(y_mm, B * TC)
                gate_up(b, c, c)

            first_half(act, {"XT": xt, "AQ": square_attention_weights, "AT": attention_weights, "F": f, "I": i,
                             "G": g, "O": o, "GU": start_second, "YN": yn, "ZT": zt,
                             "WN": wn, "WT": wt, "W2N": w2n, "H2": h2})

            def norm_out(b, t):
                act.activation(yv[:, t], yv[:, t], ACT.Identity, bias=ab[:, t, 1:2], scale=rstd[:, 1, t:t + 1]
                               ).then_inc(v_norm, 1)

            def batch_row(b, last):
                with act.Fori(0, HC // 2 - 1) as j:
                    c = 2 * j + 1
                    gate_up(b, c + 1, 0)
                    gate_up(b, c + 2, 1)
                if not last:
                    gate_up(b + 1, 0, 0)
                    gate_up(b + 1, 1, 1)
                    act.wait_ge(v_ab, b + 1)
                for t in range(TC):
                    if last:
                        act.wait_ge(v_ab, b + t + 1)
                    norm_out(b, t)

            with act.Fori(0, B - 1) as b:
                batch_row(b, False)
            batch_row(B - 1, True)

        @block.vector
        def _(dve):
            dve.memset(ones[:], 1.0).then_inc(ones_set, 1)
            dve.memset(neg_half[:], -0.5).then_inc(half_set, 1)

            def exponent_scales(sem_, base, norm, exp, s, inv, done, done_at, less=0):
                dve.tensor_scalar(exp.bitcast(I32), norm.bitcast(I32), 24, None, ALU.logical_shift_right
                                  ).then_inc(sem_, 1)
                dve.wait_ge(sem_, base + 1)
                dve.tensor_scalar(exp.bitcast(I32), exp.bitcast(I32), float(F_LEAST), None, ALU.max
                                  ).then_inc(sem_, 1)
                dve.wait_ge(sem_, base + 2)
                dve.tensor_scalar(inv.bitcast(I32), exp.bitcast(I32), BIT, (127 - ROW_EXP) * BIT, ALU.mult, ALU.add
                                  ).then_inc(sem_, 1)
                dve.tensor_scalar(s.bitcast(I32), exp.bitcast(I32), -BIT, (127 + ROW_EXP - less) * BIT,
                                  ALU.mult, ALU.add).then_inc(done, 1)
                dve.wait_ge(done, done_at)

            def row_stats(sem_, base, src, which, t):
                dve.bn_stats(st[:, which], src).then_inc(sem_, 1)
                dve.drain()
                dve.bn_aggr(mv[:, which, t], st[:, which]).then_inc(sem_, 1)
                dve.wait_ge(sem_, base + 2)

            def x1(b, t):
                m = TC * b + t
                dve.wait_ge(ld_x[t % 2], 16 * (slot_uses(b, t) + 1))
                row_stats(x_chain, 2 * m, x_in[:, t % 2], 0, t)
                dve.tensor_scalar(var[:, 0, t:t + 1], mv[:, 0, t, 1:2], EPS, 2.0 ** (-2 * X_EXP), ALU.add, ALU.mult
                                  ).then_inc(x_var, 1)

            def x2(b, t):
                m = TC * b + t
                dve.wait_ge(x_rstd, m + 1)
                dve.tensor_scalar(x_in[:, t % 2], x_in[:, t % 2], mv[:, 0, t, 0:1], rstd[:, 0, t:t + 1],
                                  ALU.subtract, ALU.mult).then_inc(x_norm, 1)

            def xt(b, t):
                dve.wait_ge(xt_hi, TC * b + t + 1)
                dve.tensor_tensor(xnt[:, 1, :, t * P:(t + 1) * P], quarters(bank("XT", b, t)),
                                  xnt[:, 0, :, t * P:(t + 1) * P], ALU.subtract).then_inc(xt_lo, 1)

            def split_attention_weights(b, w):
                for c in range(KC):
                    scale_c = c if w < 3 else 0
                    dve.wait_ge(aw_hi, KC * w + c + 1)
                    dve.scalar_tensor_tensor(split_w[w][:, 1, :, c * P:(c + 1) * P], staged[w][:, :, c * P:(c + 1) * P],
                                             row_s[:, w, scale_c:scale_c + 1], split_w[w][:, 0, :, c * P:(c + 1) * P],
                                             ALU.mult, ALU.subtract).then_inc(aw_lo, 1)

            def attention_scales(b, w):
                steps = chain_start[w]
                if w == 0:
                    dve.wait_ge(aw_sum, 1)
                elif w == 3:
                    dve.wait_ge(aw_sum, 2)
                    dve.tensor_reduce(s_tmp[:, 4:5], norm2[:, w], AX.X, ALU.add).then_inc(aw_chain, 1)
                else:
                    dve.wait_ge(aw_norm, KC * w)
                    dve.tensor_reduce(norm2[:, w], quarters(bank("AN", b, w)), AX.X, ALU.max).then_inc(aw_chain, 1)
                if w > 0:
                    steps += 1
                    dve.wait_ge(aw_chain, steps)
                n = KC if w < 3 else 1
                exponent_scales(aw_chain, steps, norm2[:, w] if w < 3 else s_tmp[:, 4:5], a_exp[:, 0:n],
                                row_s[:, w, 0:n], row_inv[:, w, 0:n], aw_srdy, w + 1)
                if w < 3:
                    dve.tensor_scalar(unscale[:, w], row_inv[:, w], 2.0 ** -X_EXP, None, ALU.mult
                                      ).then_inc(unscale_rdy, 1)
                else:
                    dve.tensor_tensor(y_inv[:, 0:1], s_tmp[:, 3:4], row_inv[:, w, 0:1], ALU.mult
                                      ).then_inc(coef_chain, 1)
                    dve.wait_ge(coef_chain, 8)
                    dve.tensor_tensor(y_inv[:, 1:2], y_inv[:, 0:1], y_inv[:, 0:1], ALU.mult).then_inc(yinv_rdy, 1)
                    dve.wait_ge(yinv_rdy, 1)

            def gate_coefficients(b, t):
                dve.wait_ge(ld_gw, 16)
                dve.tensor_tensor(g_coef[:], row_inv[:, 1], row_inv[:, 2], ALU.mult).then_inc(coef_chain, 1)
                dve.wait_ge(coef_chain, 1)
                dve.tensor_tensor(g_coef[:], g_coef[:], gw[:], ALU.mult).then_inc(coef_chain, 1)
                dve.wait_ge(coef_chain, 2)
                dve.tensor_scalar(g_coef[:].bitcast(I32), g_coef[:].bitcast(I32), 0x7FFFFFFF, None, ALU.bitwise_and
                                  ).then_inc(coef_chain, 1)
                dve.wait_ge(coef_chain, 3)
                dve.tensor_reduce(s_tmp[:, 5:6], g_coef[:], AX.X, ALU.max).then_inc(part_max, 1)
                o_exp = 126 - NORM_BOUND_EXP + HID_EXP
                dve.wait_ge(all_max, 1)
                dve.tensor_scalar(s_tmp[:, 1:2].bitcast(I32), s_tmp[:, 7:8].bitcast(I32), 23, None,
                                  ALU.logical_shift_right).then_inc(coef_chain, 1)
                dve.wait_ge(coef_chain, 4)
                dve.tensor_scalar(s_tmp[:, 2:3].bitcast(I32), s_tmp[:, 1:2].bitcast(I32), -BIT, (127 + o_exp) * BIT,
                                  ALU.mult, ALU.add).then_inc(coef_chain, 1)
                dve.tensor_scalar(s_tmp[:, 3:4].bitcast(I32), s_tmp[:, 1:2].bitcast(I32), BIT, (127 - o_exp) * BIT,
                                  ALU.mult, ALU.add).then_inc(coef_chain, 1)
                dve.wait_ge(coef_chain, 6)
                dve.scalar_tensor_tensor(g_coef[:], gw[:], s_tmp[:, 2:3], unscale[:, 2], ALU.mult, ALU.mult
                                         ).then_inc(coef_chain, 1)
                dve.wait_ge(coef_chain, 7)
                dve.tensor_scalar(g_coef[:], g_coef[:], -1.0, None, ALU.mult).then_inc(coef_rdy, 1)
                dve.wait_ge(coef_rdy, 1)

            def i(b, c):
                n = KC * b + c
                dve.wait_ge(sgi_rdy, n + 1)
                dve.scalar_tensor_tensor(sl[:], ps[gate_bank[c % 2][1]][:], unscale[:, 1, c:c + 1], sg[:, 0],
                                         ALU.mult, ALU.mult).then_inc(sli_rdy, 1)
                dve.wait_ge(sli_rdy, n + 1)
                dve.wait_ge(gate_rdy, n + 1)
                dve.scalar_tensor_tensor(sl[:], gate[:], 1.0, sl[:], ALU.subtract, ALU.mult
                                         ).then_inc(nv_rdy, 1)
                dve.wait_ge(nv_rdy, n + 1)
                if not (first(b) and c < 2):
                    dve.wait_ge(osq_rdy, n - 1)
                dve.tensor_tensor_scan(o_s[:, c % 2], gate[:], sl[:], 0.0, ALU.mult, ALU.add
                                       ).then_inc(o_rdy, 1)

            def g(b, c):
                n = KC * b + c
                dve.wait_ge(sgg_rdy, n + 1)
                if not (first(b) and c < 2):
                    dve.wait_ge(o_lo, n - 1)
                dve.scalar_tensor_tensor(gs[:, c % 2], ps[gate_bank[c % 2][2]][:], g_coef[:, c:c + 1], sg[:, 1],
                                         ALU.mult, ALU.mult).then_inc(gs_rdy, 1)
                dve.wait_ge(gs_rdy, n + 1)
                dve.wait_ge(o_rdy, n + 1)
                dve.tensor_tensor(gs[:, c % 2], gs[:, c % 2], o_s[:, c % 2], ALU.mult).then_inc(op_rdy, 1)

            def ms(b, t):
                dve.wait_ge(ms_mm, b + 1)
                dve.tensor_scalar(ms_eps[:], ps[MEAN_BANK][:, 0:TC], EPS / D, EPS * EPS, ALU.mult, ALU.add
                                  ).then_inc(e_rdy, 1)
                dve.wait_ge(e_rdy, b + 1)

            def y(b, t):
                m = TC * b + t
                dve.wait_ge(y_mm, m + 1)
                row_stats(y_chain, 2 * m, ps[t][:], 1, t)
                dve.scalar_tensor_tensor(var[:, 1, t:t + 1], mv[:, 1, t, 1:2], y_inv[:, 1:2], ms_eps[:, t:t + 1],
                                         ALU.mult, ALU.add).then_inc(y_var, 1)

            def yn(b, t):
                m = TC * b + t
                dve.wait_ge(y_rstd, m + 1)
                dve.tensor_scalar(ab[:, t, 0:1], rstd[:, 1, t:t + 1], y_inv[:, 0:1], None, ALU.mult
                                  ).then_inc(y_scale, 1)
                dve.wait_ge(y_scale, m + 1)
                dve.scalar_tensor_tensor(ab[:, t, 1:2], mv[:, 1, t, 0:1], -1.0, ab[:, t, 0:1], ALU.mult, ALU.mult
                                         ).then_inc(y_ab, 1)

            def z1(b, t):
                m = TC * b + t
                dve.wait_ge(x1_rdy, m + 1)
                row_stats(z_chain, 2 * m, x_res[:, t], 2, t)
                dve.tensor_scalar(var[:, 2, t:t + 1], mv[:, 2, t, 1:2], EPS, 2.0 ** (-2 * X_EXP), ALU.add, ALU.mult
                                  ).then_inc(z_var, 1)

            def z2(b, t):
                m = TC * b + t
                dve.wait_ge(z_rstd, m + 1)
                dve.tensor_scalar(zn[:, t], x_res[:, t], mv[:, 2, t, 0:1], rstd[:, 2, t:t + 1],
                                  ALU.subtract, ALU.mult).then_inc(z_norm, 1)

            def zt(b, t):
                dve.wait_ge(z_hi, TC * b + t + 1)
                dve.tensor_tensor(x1t_st[:, t % 2, 1], quarters(bank("ZT", b, t)), x1t_st[:, t % 2, 0], ALU.subtract
                                  ).then_inc(z_lo, 1)

            def ws(b, t):
                m = HQ * b + t
                dve.wait_ge(w_sum, m + 1)
                if not (first(b) and t == 0):
                    dve.wait_ge(wt_hi, 2 * m)
                    dve.wait_ge(wt_lo, m)
                exponent_scales(w_chain, 3 * m, wsum[:], wexp[:], w_s[:], w13_inv[:, :, bass.ds(m, 1)].squeeze(2),
                                w_srdy, m + 1)

            def wt(b, t):
                m = HQ * b + t
                for w, w_t in enumerate((w1t, w3t)):
                    dve.wait_ge(wt_hi, 2 * m + w + 1)
                    last = dve.scalar_tensor_tensor(w_t[:, 1, :, bass.ds(m * P, P)], w_tr[:, t % 2, w], w_s[:, w:w + 1],
                                                    w_t[:, 0, :, bass.ds(m * P, P)], ALU.mult, ALU.subtract)
                last.then_inc(wt_lo, 1)

            def w2s(b, t):
                m = UB * b + t
                dve.wait_ge(w2_sum, m + 1)
                exponent_scales(w2_chain, 3 * m, w2n2[:, 1:2], w2exp[:], w2_s[:, t:t + 1], w2_inv[:, bass.ds(m, 1)],
                                w2_srdy, m + 1, less=5)

            def h2(b, t):
                dve.wait_ge(h2_hi, 2 * UB * b + t + 1)
                dst = w2_dst(b, t)
                dve.scalar_tensor_tensor(dst[:, 1], h2_src(b, t), w2_s[:, t // 2:t // 2 + 1], dst[:, 0],
                                         ALU.mult, ALU.subtract).then_inc(h2_lo, 1)

            def gate_up(b, c, s):
                n = HC * b + c
                dve.wait_ge(sga_rdy, n + 1)
                dve.scalar_tensor_tensor(sil[:, s], ps[4 + s][:], gate_c[:, bass.ds(c, 1)], sga[:, s],
                                         ALU.mult, ALU.mult).then_inc(sil_rdy, 1)
                dve.wait_ge(sil_rdy, n + 1)
                dve.wait_ge(up_mm, n + 1)
                if not (isinstance(n, int) and n < 2):
                    dve.wait_ge(hid_lo, n - 1)
                dve.scalar_tensor_tensor(hd[:, s], ps[6 + s][:], up_c[:, bass.ds(c, 1)], sil[:, s],
                                         ALU.mult, ALU.mult).then_inc(hid_rdy, 1)

            def hidden_scale(b, t):
                dve.tensor_tensor(up_c[:], w13_inv[:, 0], w13_inv[:, 1], ALU.mult).then_inc(h_chain, 1)
                dve.wait_ge(h_chain, 1)
                dve.tensor_reduce(hid_s[:, 0:1], up_c[:], AX.X, ALU.max).then_inc(hid_part, 1)
                dve.wait_ge(hid_max, 1)
                dve.tensor_scalar(hid_s[:, 2:3].bitcast(I32), hid_s[:, 1:2].bitcast(I32), -1.0,
                                  (2 * 127 - NORM_BOUND_EXP + HID_EXP) * BIT, ALU.mult, ALU.add).then_inc(h_chain, 1)
                dve.wait_ge(h_chain, 2)
                dve.tensor_scalar(up_c[:], w13_inv[:, 1], hid_s[:, 2:3], 2.0 ** -X_EXP, ALU.mult, ALU.mult
                                  ).then_inc(hid_scale, 1)
                dve.tensor_scalar(gate_c[:], w13_inv[:, 0], 2.0 ** -X_EXP, None, ALU.mult).then_inc(hid_scale, 1)

            def start_second(b, c):
                if c == 0:
                    dve.wait_ge(hid_scale, 2)
                    dve.wait_ge(y_mm, B * TC)
                gate_up(b, c, c)

            first_half(dve, {"X1": x1, "X2": x2, "XT": xt, "AR": attention_scales, "AN": attention_scales,
                             "AT": split_attention_weights, "GC": gate_coefficients,
                             "I": i, "G": g, "HS": hidden_scale, "GU": start_second,
                             "MS": ms, "Y": y, "YN": yn, "Z1": z1, "Z2": z2, "ZT": zt,
                             "WS": ws, "WT": wt, "W2S": w2s, "H2": h2})

            def unscale_out(b, t):
                dve.tensor_tensor(yv[:, t], ps[t][:], row_c[:], ALU.mult).then_inc(y_free, 1)

            def out_shift(t0, t1):
                dve.scalar_tensor_tensor(ab[:, t0:t1, 1], mv[:, 1, t0:t1, 0], -1.0, rstd[:, 1, t0:t1],
                                         ALU.mult, ALU.mult).then_inc(v_ab, 1)

            def out_var(t0, t1):
                dve.tensor_scalar(var[:, 1, t0:t1], mv[:, 1, t0:t1, 1], EPS, None, ALU.add).then_inc(v_var, 1)

            def norm_out(b):
                for t in range(TC):
                    dve.wait_ge(y_free, TC * b + t + 2)
                    row_stats(v_chain, 2 * (TC * b + t), yv[:, t], 1, t)
                out_var(0, TC)
                dve.wait_ge(v_rstd, b + 1)
                out_shift(0, TC)

            def last_out(b, t):
                if t < TC:
                    dve.wait_ge(d_mm, HC * (b + 1) + t)
                    unscale_out(b, t)
                    dve.wait_ge(y_free, TC * b + t + 2)
                    row_stats(v_chain, 2 * (TC * b + t), yv[:, t], 1, t)
                    out_var(t, t + 1)
                if 1 <= t <= TC:
                    dve.wait_ge(v_rstd, b + t)
                    out_shift(t - 1, t)
                if t >= 2:
                    dve.wait_ge(v_norm, TC * b + t - 1)
                    dve.tensor_tensor(yv[:, t - 2], yv[:, t - 2], x1r[:, t - 2], ALU.add).then_inc(out_last, 1)

            def batch_row(b, last):
                with dve.Fori(0, HC // 2 - 1) as j:
                    c = 2 * j + 1
                    gate_up(b, c + 1, 0)
                    gate_up(b, c + 2, 1)
                if not last:
                    gate_up(b + 1, 0, 0)
                dve.wait_ge(ld_x1r, 16 * (b + 1))
                if last:
                    for t in range(TC + 2):
                        last_out(b, t)
                else:
                    dve.wait_ge(d_mm, HC * (b + 1))
                    for t in range(TC):
                        unscale_out(b, t)
                    gate_up(b + 1, 1, 1)
                    norm_out(b)

            dve.wait_ge(o_lo, B * KC)
            dve.wait_ge(x1_rdy, B * TC)
            dve.wait_ge(z_mm, B * TC)
            for slot in range(2):
                dve.wait_ge(st_x1t[slot], 16 * slot_uses(B, 0))
            for t in range(TC):
                dve.wait_ge(st_x1[t], 16 * B)

            out_scale = 2.0 ** (NORM_BOUND_EXP - HID_EXP + 5) * float(np.float32(1.0 / np.sqrt(H)))
            dve.tensor_scalar(w2_inv[:], w2_inv[:], hid_s[:, 1:2], out_scale, ALU.mult, ALU.mult
                              ).then_inc(h_chain, 1)
            dve.wait_ge(h_chain, 3)
            dve.tensor_copy(row_c[:].rearrange("p (u d) -> p u d", d=UW),
                            w2_inv[:].rearrange("p (u o) -> p u o", o=1).broadcast_to((P, UNITS, UW))
                            ).then_inc(y_free, 1)
            dve.wait_ge(y_free, 1)
            with dve.Fori(0, B - 1) as b:
                batch_row(b, False)
            batch_row(B - 1, True)

        @block.gpsimd
        def _(pool):
            def rsqrt(dst, src, done):
                pool.tensor_tensor(dst, src, neg_half[:].broadcast_to(src.shape), ALU.pow).then_inc(done, 1)

            def x1(b, t):
                pool.wait_ge(x_var, TC * b + t + 1)
                if first(b) and t == 0:
                    pool.wait_ge(half_set, 1)
                    pool.wait_ge(ones_set, 1)
                rsqrt(rstd[:, 0, t:t + 1], var[:, 0, t:t + 1], x_rstd)

            def square_attention_weights(b, w):
                if w == 2:
                    pool.wait_ge(ld_aw[w], 16)
                    for k in range(KC):
                        pool.wait_ge(aw_sq_act, k + 1)
                        pool.tensor_tensor(g_squares[k], staged[w][:, k], staged[w][:, k], ALU.mult
                                           ).then_inc(aw_sq, 1)

            def sum_attention_weights(b, w):
                pool.wait_ge(aw_sq_act, KC if w == 0 else 3 * KC)
                pool.partition_all_reduce(norm2[:, w], norm2_part[:, w // 3], P, RSUM).then_inc(aw_sum, 1)

            def gate_coefficients(b, t):
                pool.wait_ge(part_max, 1)
                pool.partition_all_reduce(s_tmp[:, 7:8], s_tmp[:, 5:6], P, RMAX).then_inc(all_max, 1)

            def o(b, c):
                n = KC * b + c
                if c > 0:
                    pool.wait_ge(osq_rdy, n + 1)
                    pool.wait_ge(oadd, (KC - 1) * b + c - 1)
                    pool.tensor_tensor(osum[:], osum[:], osq[:], ALU.add).then_inc(oadd, 1)
                pool.wait_ge(o_hi, n + 1)
                pool.tensor_tensor(ot[:, 1, c, :], gs[:, c % 2], ot[:, 0, c, :], ALU.subtract).then_inc(o_lo, 1)

            def y(b, t):
                pool.wait_ge(y_var, TC * b + t + 1)
                rsqrt(rstd[:, 1, t:t + 1], var[:, 1, t:t + 1], y_rstd)

            def yn(b, t):
                pool.wait_ge(y_norm, TC * b + t + 1)
                pool.wait_ge(ld_res[t], 16 * (b + 1))
                pool.tensor_tensor(x_res[:, t], x_res[:, t], zn[:, t], ALU.add).then_inc(x1_rdy, 1)

            def z1(b, t):
                pool.wait_ge(z_var, TC * b + t + 1)
                rsqrt(rstd[:, 2, t:t + 1], var[:, 2, t:t + 1], z_rstd)

            def wn(b, t):
                m = HQ * b + t
                pool.wait_ge(w_sq, 2 * (m + 1))
                if not (first(b) and t == 0):
                    pool.wait_ge(w_srdy, m)
                pool.tensor_tensor(wn2_in[:], wn2[:], ones[:, 0:2], ALU.mult)
                pool.drain()
                pool.partition_all_reduce(wsum[:], wn2_in[:], P, RSUM).then_inc(w_sum, 1)

            def w2n(b, t):
                m = UB * b + t
                pool.wait_ge(w2_sq, m + 1)
                if not (first(b) and t == 0):
                    pool.wait_ge(w2_srdy, m)
                pool.tensor_tensor(w2n2[:, 2:3], w2n2[:, 0:1], ones[:, 0:1], ALU.mult)
                pool.drain()
                pool.partition_all_reduce(w2n2[:, 1:2], w2n2[:, 2:3], P, RSUM).then_inc(w2_sum, 1)

            def fly(b, k):
                m, stage, half = UB * b + k // 8, k % 8 // 2, k % 2
                start, other = w2_bufs[k // 8], w2_bufs[1 - k // 8]
                if k == 0 and first(b):
                    pool.wait_ge(aw_norm, 2 * KC)
                    pool.wait_ge(aw_sq_act, 3 * KC)
                elif k % 8 == 0:
                    pool.wait_ge(h2_mm, 2 * m)
                if k % 8 == 0:
                    pool.wait_ge(ld_w2[k // 8], 16 * (b + 1))
                elif half == 0:
                    pool.wait_ge(w2_fly, 8 * UB * b + k)
                if k % 8 == 2:
                    pool.wait_ge(w2_sq, m + 1)
                src, dst = (start, other) if stage % 2 == 0 else (other, start)
                s, d = (v[:].rearrange("p (g two w) d -> p g two (w d)", two=2, w=1 << stage) for v in (src, dst))
                pool.tensor_tensor(d[:, :, half], s[:, :, 0], s[:, :, 1], ALU.subtract if half else ALU.add
                                   ).then_inc(w2_fly, 1)

            def hidden_scale(b, t):
                pool.wait_ge(hid_part, 1)
                pool.partition_all_reduce(hid_s[:, 1:2], hid_s[:, 0:1], P, RMAX).then_inc(hid_max, 1)

            def split(b, c, s):
                n = HC * b + c
                pool.wait_ge(hid_hi, n + 1)
                pool.tensor_tensor(hsp[:, s, 1], hd[:, s], hsp[:, s, 0], ALU.subtract).then_inc(hid_lo, 1)

            first_half(pool, {"X1": x1, "AQ": square_attention_weights, "AR": sum_attention_weights,
                              "GC": gate_coefficients, "O": o, "HS": hidden_scale,
                              "GU": lambda b, c: split(b, c, c), "Y": y, "YN": yn, "Z1": z1, "WN": wn,
                              "W2N": w2n, "FW": fly})

            def residual(b):
                pool.wait_ge(v_var, b + 1)
                rsqrt(rstd[:, 1], var[:, 1], v_rstd)
                pool.wait_ge(ld_x1r, 16 * (b + 1))
                for t in range(TC):
                    pool.wait_ge(v_norm, TC * b + t + 1)
                    pool.tensor_tensor(yv[:, t], yv[:, t], x1r[:, t], ALU.add).then_inc(out_rdy, 1)

            def batch_row(b, last):
                with pool.Fori(0, HC // 2 - 1) as j:
                    c = 2 * j + 1
                    split(b, c + 1, 0)
                    split(b, c + 2, 1)
                if last:
                    for t in range(TC):
                        pool.wait_ge(v_var, b + t + 1)
                        rsqrt(rstd[:, 1, t:t + 1], var[:, 1, t:t + 1], v_rstd)
                else:
                    split(b + 1, 0, 0)
                    split(b + 1, 1, 1)
                    residual(b)

            with pool.Fori(0, B - 1) as b:
                batch_row(b, False)
            batch_row(B - 1, True)


_INS = ["L0_attn_hidden_states", "L0_attn_Wi", "L0_attn_Wf", "L0_attn_Wg", "L0_attn_Wo", "L0_attn_gnorm_w",
        "L0_ffn_W1", "L0_ffn_W2", "L0_ffn_W3"]


def kernel(**inputs):
    import concourse.bacc as bacc
    from concourse.bass_utils import run_bass_kernel_spmd

    nc = bacc.Bacc("TRN2", target_bir_lowering=False, num_devices=1)
    sign = np.ones((1, 1), np.float32)
    while sign.shape[0] < P:
        sign = np.block([[sign, sign], [sign, -sign]])
    arrays = {name: np.ascontiguousarray(inputs[name]) for name in _INS}
    arrays["gnorm"] = np.ascontiguousarray(arrays.pop("L0_attn_gnorm_w").reshape(-1, P).T)
    arrays["eye"] = np.eye(P, dtype=np.float32)
    arrays["hadamard"] = np.ascontiguousarray(sign)
    for name in ("Wf", "Wi", "Wg", "Wo"):
        w = arrays["L0_attn_" + name]
        arrays["L0_attn_" + name] = np.ascontiguousarray(w.T.reshape(-1, P, w.shape[0]).transpose(1, 0, 2))
    w_13 = np.stack([arrays.pop("L0_ffn_W1"), arrays.pop("L0_ffn_W3")])
    hc, kc = w_13.shape[1] // P, w_13.shape[2] // P
    arrays["W13t"] = np.ascontiguousarray(w_13.reshape(2, hc, P, kc, P).transpose(1, 4, 0, 3, 2))
    arrays["W2t"] = np.ascontiguousarray(
        arrays.pop("L0_ffn_W2").reshape(-1, UNIT_WIDTH, hc, P).transpose(0, 3, 2, 1))
    aps = {name: nc.dram_tensor(name, a.shape, mybir.dt.from_np(a.dtype), kind="ExternalInput").ap()
           for name, a in arrays.items()}
    out = nc.dram_tensor("out", arrays[_INS[0]].shape, F32, kind="ExternalOutput").ap()
    mixer_ffn_kernel(nc, aps["L0_attn_hidden_states"], aps["L0_attn_Wi"], aps["L0_attn_Wf"], aps["L0_attn_Wg"],
                     aps["L0_attn_Wo"], aps["gnorm"], aps["W13t"], aps["W2t"], aps["eye"], aps["hadamard"], out)
    results = run_bass_kernel_spmd(nc, [arrays], core_ids=[0])
    return results.results[0]["out"]
```
